# Optimizing a Trainium2 kernel written in Bass

```python
import numpy as np
import jax
import jax.numpy as jnp

def _softmax(x, axis=-1):
    return jax.nn.softmax(x, axis=axis)

def _gelu(x):
    return jax.nn.gelu(x, approximate=True)

def _silu(x):
    return jax.nn.silu(x)

def _sigmoid(x):
    return jax.nn.sigmoid(x)

def _layernorm(x, axis=-1, eps=1e-05):
    m = jnp.mean(x, axis=axis, keepdims=True)
    v = jnp.var(x, axis=axis, keepdims=True)
    return (x - m) / jnp.sqrt(v + eps)

def _scatter_add(tgt, idx, src, axis=0):
    return tgt.at[idx].add(src)

def _segment_sum(src, seg, n):
    return jax.ops.segment_sum(src, seg, n)
kernel_name = 'mk_macaron_d1_jaxref_r8_e97e4c'

def setup_inputs(seed: int=0):
    np.random.seed(seed)
    _w = jnp.asarray

    def _L0_attn_setup():
        import jax, jax.numpy as jnp
        import numpy as np
        EMB_DIM = 256
        NUM_HEADS = 16
        HEAD_DIM = EMB_DIM // NUM_HEADS
        B, T = (4, 256)
        key = jax.random.key(seed)
        ks = jax.random.split(key, 6)
        s = lambda fan_in: 1.0 / np.sqrt(fan_in)
        return {'x': jax.random.normal(ks[0], (B, T, EMB_DIM), dtype=jnp.float32), 'Wq': jax.random.normal(ks[1], (EMB_DIM, EMB_DIM), dtype=jnp.float32) * s(EMB_DIM), 'Wk': jax.random.normal(ks[2], (EMB_DIM, HEAD_DIM), dtype=jnp.float32) * s(EMB_DIM), 'Wv': jax.random.normal(ks[3], (EMB_DIM, HEAD_DIM), dtype=jnp.float32) * s(EMB_DIM), 'Wo': jax.random.normal(ks[4], (EMB_DIM, EMB_DIM), dtype=jnp.float32) * s(EMB_DIM), 'bo': jax.random.normal(ks[5], (EMB_DIM,), dtype=jnp.float32) * 0.01}
    _L0_attn_in = _L0_attn_setup()

    def _L0_ffn_setup():
        import jax, jax.numpy as jnp
        import numpy as np
        NUM_EXPERTS = 32
        TOP_K = 8
        SELECT_TOP_K = 4
        THRESHOLD = 0.5
        HIDDEN = 256
        D_FF = 96

        def _moe_forward(hidden_states, gate_weight, gate_up_proj, down_proj, similarity):
            B, S_len, H = hidden_states.shape
            E, K, Ssel = (NUM_EXPERTS, TOP_K, SELECT_TOP_K)
            x = hidden_states.reshape(-1, H)
            router_logits = x @ gate_weight.T
            router_probs = jax.nn.softmax(router_logits.astype(jnp.float32), axis=-1).astype(router_logits.dtype)
            router_top_value, router_indices = jax.lax.top_k(router_probs, K)
            routing_weights = router_top_value / jnp.clip(jnp.sum(router_top_value, axis=-1, keepdims=True), 1e-12, None)
            sim = similarity.astype(jnp.float32)
            sim = sim.at[jnp.arange(E), jnp.arange(E)].set(1.0)
            prim = router_indices[:, :Ssel]
            sec = router_indices[:, Ssel:]
            sim_cand = sim[sec[:, :, None], prim[:, None, :]]
            best_sim = jnp.max(sim_cand, axis=-1)
            best_i = jnp.argmax(sim_cand, axis=-1)
            prim_rep = jnp.broadcast_to(prim[:, None, :], sim_cand.shape)
            best_primary = jnp.take_along_axis(prim_rep, best_i[..., None], axis=-1)[..., 0]
            new_sec = jnp.where(best_sim < THRESHOLD, sec, best_primary) if THRESHOLD > 0.0 else best_primary
            rerouted_indices = jnp.concatenate([prim, new_sec], axis=1)
            combine = jnp.sum(jax.nn.one_hot(rerouted_indices, E, dtype=routing_weights.dtype) * routing_weights[..., None], axis=1)

            def expert_step(y, params):
                wgu, wd, cw = params
                gu = x @ wgu.T
                g, u = jnp.split(gu, 2, axis=-1)
                h = jax.nn.silu(g) * u
                y = y + h @ wd.T * cw[:, None]
                return (y, None)
            y0 = jnp.zeros_like(x)
            y, _ = jax.lax.scan(expert_step, y0, (gate_up_proj, down_proj, combine.T))
            return y.reshape(B, S_len, H)
        key = jax.random.key(seed)
        ks = jax.random.split(key, 5)
        hidden_states = jax.random.normal(ks[0], (4, 256, HIDDEN), dtype=jnp.float32)
        gate_weight = jax.random.normal(ks[1], (NUM_EXPERTS, HIDDEN), dtype=jnp.float32) * 0.02
        gate_up_proj = jax.random.normal(ks[2], (NUM_EXPERTS, 2 * D_FF, HIDDEN), dtype=jnp.float32) * 0.02
        down_proj = jax.random.normal(ks[3], (NUM_EXPERTS, HIDDEN, D_FF), dtype=jnp.float32) * 0.02
        similarity = jax.random.uniform(ks[4], (NUM_EXPERTS, NUM_EXPERTS), dtype=jnp.float32)
        return {'hidden_states': hidden_states, 'gate_weight': gate_weight, 'gate_up_proj': gate_up_proj, 'down_proj': down_proj, 'similarity': similarity}
    _L0_ffn_in = _L0_ffn_setup()
    _d = {'L0_attn_x': _L0_attn_in['x'], 'L0_attn_Wq': _L0_attn_in['Wq'], 'L0_attn_Wk': _L0_attn_in['Wk'], 'L0_attn_Wv': _L0_attn_in['Wv'], 'L0_attn_Wo': _L0_attn_in['Wo'], 'L0_attn_bo': _L0_attn_in['bo'], 'L0_ffn_gate_weight': _L0_ffn_in['gate_weight'], 'L0_ffn_gate_up_proj': _L0_ffn_in['gate_up_proj'], 'L0_ffn_down_proj': _L0_ffn_in['down_proj'], 'L0_ffn_similarity': _L0_ffn_in['similarity']}
    _x0 = _d['L0_attn_x']
    _d['L0_attn_x'] = jax.random.normal(jax.random.fold_in(jax.random.key(seed), 1), (4, 256, 256), dtype=_x0.dtype)
    del _x0
    return _d

def reference(L0_attn_x, L0_attn_Wq, L0_attn_Wk, L0_attn_Wv, L0_attn_Wo, L0_attn_bo, L0_ffn_gate_weight, L0_ffn_gate_up_proj, L0_ffn_down_proj, L0_ffn_similarity):

    def _L0_attn_ref(x, Wq, Wk, Wv, Wo, bo):
        import jax, jax.numpy as jnp
        import numpy as np
        EMB_DIM = 256
        NUM_HEADS = 16
        HEAD_DIM = EMB_DIM // NUM_HEADS
        B, T = (4, 256)
        Bsz, Tlen, C = x.shape
        H, D = (NUM_HEADS, HEAD_DIM)
        q = (x @ Wq).reshape(Bsz, Tlen, H, D)
        k = x @ Wk
        v = x @ Wv
        scores = jnp.einsum('bihd,bjd->bhij', q, k) / jnp.sqrt(jnp.float32(D))
        i = jnp.arange(Tlen)[:, None]
        j = jnp.arange(Tlen)[None, :]
        causal = j <= i
        scores = jnp.where(causal, scores, -jnp.inf)
        attn = jax.nn.softmax(scores, axis=-1)
        out = jnp.einsum('bhij,bjd->bihd', attn, v).reshape(Bsz, Tlen, C)
        return out @ Wo + bo

    def _L0_ffn_ref(hidden_states, gate_weight, gate_up_proj, down_proj, similarity):
        import jax, jax.numpy as jnp
        import numpy as np
        NUM_EXPERTS = 32
        TOP_K = 8
        SELECT_TOP_K = 4
        THRESHOLD = 0.5
        HIDDEN = 256
        D_FF = 96

        def _moe_forward(hidden_states, gate_weight, gate_up_proj, down_proj, similarity):
            B, S_len, H = hidden_states.shape
            E, K, Ssel = (NUM_EXPERTS, TOP_K, SELECT_TOP_K)
            x = hidden_states.reshape(-1, H)
            router_logits = x @ gate_weight.T
            router_probs = jax.nn.softmax(router_logits.astype(jnp.float32), axis=-1).astype(router_logits.dtype)
            router_top_value, router_indices = jax.lax.top_k(router_probs, K)
            routing_weights = router_top_value / jnp.clip(jnp.sum(router_top_value, axis=-1, keepdims=True), 1e-12, None)
            sim = similarity.astype(jnp.float32)
            sim = sim.at[jnp.arange(E), jnp.arange(E)].set(1.0)
            prim = router_indices[:, :Ssel]
            sec = router_indices[:, Ssel:]
            sim_cand = sim[sec[:, :, None], prim[:, None, :]]
            best_sim = jnp.max(sim_cand, axis=-1)
            best_i = jnp.argmax(sim_cand, axis=-1)
            prim_rep = jnp.broadcast_to(prim[:, None, :], sim_cand.shape)
            best_primary = jnp.take_along_axis(prim_rep, best_i[..., None], axis=-1)[..., 0]
            new_sec = jnp.where(best_sim < THRESHOLD, sec, best_primary) if THRESHOLD > 0.0 else best_primary
            rerouted_indices = jnp.concatenate([prim, new_sec], axis=1)
            combine = jnp.sum(jax.nn.one_hot(rerouted_indices, E, dtype=routing_weights.dtype) * routing_weights[..., None], axis=1)

            def expert_step(y, params):
                wgu, wd, cw = params
                gu = x @ wgu.T
                g, u = jnp.split(gu, 2, axis=-1)
                h = jax.nn.silu(g) * u
                y = y + h @ wd.T * cw[:, None]
                return (y, None)
            y0 = jnp.zeros_like(x)
            y, _ = jax.lax.scan(expert_step, y0, (gate_up_proj, down_proj, combine.T))
            return y.reshape(B, S_len, H)
        return _moe_forward(hidden_states, gate_weight, gate_up_proj, down_proj, similarity)
    x = L0_attn_x
    x = x + 0.5 * _L0_ffn_ref(_layernorm(x, axis=-1), L0_ffn_gate_weight, L0_ffn_gate_up_proj, L0_ffn_down_proj, L0_ffn_similarity)
    x = x + _L0_attn_ref(_layernorm(x, axis=-1), L0_attn_Wq, L0_attn_Wk, L0_attn_Wv, L0_attn_Wo, L0_attn_bo)
    x = x + 0.5 * _L0_ffn_ref(_layernorm(x, axis=-1), L0_ffn_gate_weight, L0_ffn_gate_up_proj, L0_ffn_down_proj, L0_ffn_similarity)
    return x

_drawn_inputs = setup_inputs


def setup_inputs(seed=0):
    import zlib

    import numpy as np

    out = dict(_drawn_inputs(seed))
    spreads = {}
    factors = {'L0_attn_bo': 5.537,
     'L0_ffn_gate_weight': 8.0,
     'L0_ffn_gate_up_proj': 8.0,
     'L0_ffn_down_proj': 8.0,
     'L0_ffn_similarity': 8.0}
    for name, (base, spread) in spreads.items():
        noise = np.random.default_rng([zlib.crc32(name.encode()), seed]).standard_normal(out[name].shape)
        drawn = base * np.exp(spread * noise) if base else spread * noise
        out[name] = jnp.asarray(drawn.astype(out[name].dtype))
    for name, factor in factors.items():
        out[name] = (out[name] * factor).astype(out[name].dtype)
    return out
```

```python
import concourse.bass as bass
from concourse import mybir
from contextlib import ExitStack

P = 128
B, T, C = 4, 256, 256
NT = B * T // P
BT = T // P
KC = C // P
E, F = 32, 96
TOP, PRIM = 8, 4
SEC = TOP - PRIM
H, D = 16, 16
HB = P // D
EG = 4
G = E // EG
GC = EG * 2 * F
HC = GC // 2
FC = EG * F // P
RB = GC // P
UNITS = G * NT
STEPS = RB // 2 + FC
BIG = -1.0e30
EPS = 1e-5
RING = 3
HP = H // 2
MOVES = 3 * (H // HB)

SCRATCH = {"GW": (2,), "LN": (0,), "R1": (2,), "R2": (0, 1), "QK": (1, 2), "SM": (2,), "PV": (), "OU": (0, 1)}
CHUNKS = {"SM": H // 4 + H // 2, "PV": 2 * HP}

PROLOGUE = [("GW", 0), ("LN", 0), ("LN", 1), ("LN", 2), ("LN", 3), ("PREP", 0),
            ("R1", 0), ("R1", 1), ("R2", 0), ("R1", 2), ("R2", 1), ("R1", 3), ("R2", 2), ("R2", 3)]
ATTENTION = [("LN", 4), ("QK", 0), ("LN", 5), ("QK", 1), ("SM", 0),
             ("PV", 0), ("LN", 6), ("QK", 2), ("SM", 1), ("OU", 0), ("LN", 8),
             ("PV", 1), ("LN", 7), ("QK", 3), ("SM", 2), ("R1", 4), ("OU", 1), ("LN", 9),
             ("PV", 2), ("R2", 4), ("SM", 3), ("R1", 5), ("OU", 2), ("LN", 10), ("R2", 5),
             ("PV", 3), ("R1", 6), ("OU", 3), ("LN", 11), ("R2", 6), ("R1", 7), ("R2", 7)]


def place_stages():
    job, chunk, used, at = {}, {}, [0, 0, 0], 0
    for name, n in PROLOGUE + ATTENTION:
        for bank in SCRATCH.get(name, ()):
            job[name, n, bank] = used[bank]
            used[bank] += 1
        chunk[name, n] = at
        at += CHUNKS.get(name, 0)
    return job, chunk, used


JOB, CHUNK, JOBS = place_stages()
SEQ = {(name, n): [s for s in PROLOGUE + ATTENTION if s[0] == name].index((name, n)) for name, n in PROLOGUE + ATTENTION}


def ring_use(r):
    return r % RING, r // RING


def macaron(nc, x_in, wq, wk, wv, wo, bo, gate_w, gate_up, down, sim, out):
    f32, f32r, bf16, u32 = mybir.dt.float32, mybir.dt.float32r, mybir.dt.bfloat16, mybir.dt.uint32
    ALU, ACT, AX = mybir.AluOpType, mybir.ActivationFunctionType, mybir.AxisListType.X

    x_rows = x_in.rearrange("b (i p) c -> p (b i) c", p=P)
    out_rows = out.rearrange("b (i p) c -> p (b i) c", p=P)
    gate_up_rows = gate_up.rearrange("(g e) f c -> g (e f) c", g=G).rearrange("g (r p) c -> g p r c", p=P)
    down_rows = down.rearrange("(g e) (h p) f -> g h p e f", g=G, p=P)

    q_dram = nc.dram_tensor("q_dram", (B, 2, P, H // HB, T), f32, kind="Internal").ap()

    with ExitStack() as ctx:
        def sb(name, shape, dt, stack=ctx):
            return stack.enter_context(nc.sbuf_tensor(name, shape, dt))

        def sem(name):
            return ctx.enter_context(nc.semaphore(name))

        x = sb("x", [P, NT, C], f32)
        xt_hi = sb("xt_hi", [P, KC, B * T], f32r)
        xt_lo = sb("xt_lo", [P, KC, B * T], f32r)
        wgu_hi = sb("wgu_hi", [P, G, KC, GC], f32r)
        wgu_lo = sb("wgu_lo", [P, G, KC, GC], f32r)
        wd_hi = sb("wd_hi", [P, G, FC, C], f32r)
        wd_lo = sb("wd_lo", [P, G, FC, C], f32r)
        ht_hi = sb("ht_hi", [P, 2, FC * P], f32r)
        ht_lo = sb("ht_lo", [P, 2, FC * P], f32r)
        cw = sb("cw", [P, NT, E], f32)
        with ExitStack() as moe:
            raw_gu = sb("raw_gu", [P, RB, C], f32, moe)
            raw_d = sb("raw_d", [P, KC, EG, F], f32, moe)
        qs = sb("qs", [P, H, T], f32r)
        h = sb("h", [P, 2, EG, F], f32)
        probs = sb("probs", [P, 2, 3 * T], f32)
        wq_hi, wq_lo = sb("wq_hi", [P, KC, C], f32r), sb("wq_lo", [P, KC, C], f32r)
        wk_hi, wk_lo = sb("wk_hi", [P, KC, 7 * D], f32r), sb("wk_lo", [P, KC, 7 * D], f32r)
        wv_hi, wv_lo = sb("wv_hi", [P, KC, D], f32r), sb("wv_lo", [P, KC, D], f32r)
        wo_sb = sb("wo_sb", [P, KC, C], f32)
        bo_row = sb("bo_row", [1, C], f32)
        ones_row = sb("ones_row", [1, P], f32)
        ks = sb("ks", [P, T], f32r)
        v1 = sb("v1", [P, 2, BT, D + 1], f32)
        neg_max = sb("neg_max", [P, BT, H], f32)
        neg_max_t = sb("neg_max_t", [H, T], f32r)
        at = sb("at", [P, BT, C], f32)
        rsum = sb("rsum", [P, BT, H], f32)
        ident = sb("ident", [P, P], f32)
        ident_b = sb("ident_b", [P, 2 * P], bf16)
        hide_q = sb("hide_q", [P, P], bf16)
        hide_k = sb("hide_k", [P, P], bf16)
        iota = sb("iota", [P, E], f32)
        rank = sb("rank", [P, PRIM], f32)
        work = sb("work", [P, BT, C], f32)
        stats, mv = sb("stats", [P, BT, 6], f32), sb("mv", [P, BT, 2], f32)
        var_eps, rstd = sb("var_eps", [P, BT], f32), sb("rstd", [P, BT], f32)
        minus_half = sb("minus_half", [P, BT], f32)
        gw_hi, gw_lo = sb("gw_hi", [P, KC, E], f32r), sb("gw_lo", [P, KC, E], f32r)
        sim_bd = sb("sim_bd", [P, P], f32)
        pr = sb("pr", [P, BT, E], f32)
        pmax, psumm = sb("pmax", [P, BT], f32), sb("psumm", [P, BT], f32)
        top = sb("top", [P, 2, BT, TOP], f32)
        top_i, top_f = sb("top_i", [P, BT, TOP], u32), sb("top_f", [P, BT, TOP], f32)
        onehot = sb("onehot", [P, 2, BT, TOP, E], bf16)
        onehot_t = sb("onehot_t", [P, BT, P], f32)
        cand = sb("cand", [P, BT, SEC, PRIM], f32)
        pick = sb("pick", [P, BT, SEC, PRIM], f32)
        best, moved = sb("best", [P, BT, SEC], f32), sb("moved", [P, BT, SEC], f32)
        gain, slot_w = sb("gain", [P, BT, PRIM], f32), sb("slot_w", [P, BT, TOP], f32)

        def bank(name, n=1):
            return ctx.enter_context(nc.psum_tensor(name, [P, n, 512], f32))
        scratch = [bank(f"scratch{i}") for i in range(3)]
        ring0 = bank("ring0")
        pair = [bank("pair0", 2), bank("pair1", 2)]
        scr = [s[:, 0, :] for s in scratch]
        ring = [ring0[:, 0, :], pair[0][:, 0, :], pair[0][:, 1, :]]
        prep = ring0[:, 0, :]
        pv = [pair[1][:, 0, 0:H * (D + 1)], pair[1][:, 1, 0:H * (D + 1)]]

        x_loaded = [sem(f"x_loaded{b}") for b in range(B)]
        small_loaded, raw_loaded, wo_loaded = sem("small_loaded"), sem("raw_loaded"), sem("wo_loaded")
        gu_loaded, d_loaded = sem("gu_loaded"), sem("d_loaded")
        out_stored = sem("out_stored")
        pool_chain, consts_ready = sem("pool_chain"), sem("consts_ready")
        zeros_ready, attn_w_ready = sem("zeros_ready"), sem("attn_w_ready")
        dve_chain = sem("dve_chain")
        filled = [sem(f"scratch_filled{i}") for i in range(3)]
        drained = [sem(f"scratch_drained{i}") for i in range(3)]
        copied = [sem(f"scratch_copied{i}") for i in range(3)]
        ring_filled = sem("ring_filled")
        ring_drained = [sem(f"ring_drained{i}") for i in range(RING)]
        var_ready, rstd_ready = sem("var_ready"), sem("rstd_ready")
        xn_ready = sem("xn_ready")
        router_exp, onehot_ready = sem("router_exp"), sem("onehot_ready")
        cw_ready = sem("cw_ready")
        q_out = sem("q_out")
        q_moved, max_moved = sem("q_moved"), sem("max_moved")
        probs_used = sem("probs_used")
        attn_ready = sem("attn_ready")
        gu_done, silu_done, h_ready = sem("gu_done"), sem("silu_done"), sem("h_ready")
        tr_done, ht_hi_ready, ht_ready = sem("tr_done"), sem("ht_hi_ready"), sem("ht_ready")
        dn_done, x_added = sem("dn_done"), sem("x_added")
        w_transposed, w_hi_ready, w_ready = sem("w_transposed"), sem("w_hi_ready"), sem("w_ready")

        block = ctx.enter_context(nc.Block())

        def base(b):
            return 64 * (b % 2)

        def prep_parts(s):
            if s < RB // 2:
                return [(raw_gu[:, 2 * s + r, k * P:(k + 1) * P], (k * 2 + r) * P)
                        for k in range(KC) for r in range(2)]
            j = s - RB // 2
            flat = raw_d[:, :, :, :].rearrange("p k e f -> p k (e f)")
            return [(flat[:, k, j * P:(j + 1) * P], k * P) for k in range(KC)]

        def prep_out(w_gu, w_d, g, s):
            if s < RB // 2:
                return (w_gu[:, g, :, 2 * s * P:2 * (s + 1) * P],
                        prep[:, 0:4 * P].rearrange("p (k n) -> p k n", k=KC))
            return w_d[:, g, s - RB // 2, :], prep[:, 0:2 * P]

        def move_max(sp, b):
            sp.wait_ge(drained[2], JOB["SM", b, 2] + 1)
            row = base(b) + 3 * D
            sp.dma_start(qs[row:row + 1, :, :].bitcast(f32), neg_max_t[:].bitcast(f32)).then_inc(max_moved, 16)

        @block.sync
        def _(sp):
            for b in range(B):
                sp.dma_start(x[:, BT * b:BT * (b + 1), :], x_rows[:, BT * b:BT * (b + 1), :]).then_inc(x_loaded[b], 16)
            sp.dma_start(raw_gu[:], gate_up_rows[0]).then_inc(gu_loaded, 16)
            for k in range(KC):
                sp.dma_start(raw_d[:, k], down_rows[0, k]).then_inc(d_loaded, 16)
            with sp.Fori(1, G) as g:
                sp.wait_ge(w_transposed, g * STEPS - STEPS + RB // 2)
                sp.dma_start(raw_gu[:], gate_up_rows[g]).then_inc(gu_loaded, 16)
                sp.wait_ge(w_transposed, g * STEPS)
                for k in range(KC):
                    sp.dma_start(raw_d[:, k], down_rows[g, k]).then_inc(d_loaded, 16)
            for b in range(B):
                def move_q():
                    sp.wait_ge(drained[1], JOB["QK", b, 1] + 1)
                    if b == 0:
                        sp.wait_ge(w_transposed, G * STEPS)
                    if b >= 2:
                        sp.wait_ge(probs_used, HP * (b - 1))
                    for m, part in enumerate((ht_hi, ht_lo)):
                        flat = part[:, :, :].rearrange("p a n -> p (a n)")[:, 0:2 * T].bitcast(f32)
                        sp.dma_start(q_dram[b, m].rearrange("p a t -> p (a t)"), flat).then_inc(q_out, 16)
                    sp.wait_ge(q_out, 32 * (b + 1))
                    for row, m in ((0, 0), (D, 1), (2 * D, 0)):
                        for blk in range(H // HB):
                            sp.dma_start(qs[base(b) + row:base(b) + row + D, blk * HB:(blk + 1) * HB, :].bitcast(f32),
                                         q_dram[b, m, :, blk, :].rearrange("(h d) t -> d h t", d=D)).then_inc(q_moved, 16)
                move_q()
                if b >= 1:
                    move_max(sp, b - 1)
            move_max(sp, B - 1)
            for t in range(NT):
                sp.wait_ge(x_added, 2 * UNITS - NT + t + 1)
                sp.dma_start(out_rows[:, t, :], x[:, t, :]).then_inc(out_stored, 16)
            sp.wait_ge(out_stored, 16 * NT)

        @block.gpsimd
        def _(pool):
            steps = [0]

            def link(ins):
                steps[0] += 1
                ins.then_inc(pool_chain, 1)
                pool.wait_ge(pool_chain, steps[0])

            link(nc.gpsimd.memset(minus_half[:], -0.5))

            def rsqrt(n):
                pool.wait_ge(var_ready, n + 1)
                nc.gpsimd.tensor_tensor(rstd[:], var_eps[:], minus_half[:], ALU.pow).then_inc(rstd_ready, 1)

            link(nc.gpsimd.memset(ident[:], 0.0))
            link(nc.gpsimd.affine_select(out=ident[:], in_=ident[:], compare_op=ALU.not_equal, fill=1.0,
                                         base=0, pattern=[[-1, P]], channel_multiplier=1))
            link(nc.gpsimd.memset(sim_bd[:], 0.0))
            nc.gpsimd.iota(iota[:], pattern=[[1, E]], base=0, channel_multiplier=0,
                           allow_small_or_imprecise_dtypes=True).then_inc(zeros_ready, 1)
            for r in range(PRIM):
                link(nc.gpsimd.memset(rank[:, r:r + 1], float(PRIM - r)))
            link(nc.gpsimd.memset(ones_row[:], 1.0))
            link(nc.gpsimd.memset(ident_b[:, 0:P], 0.0))
            link(nc.gpsimd.tensor_copy(ident_b[:, P:2 * P], ident[:]))
            link(nc.gpsimd.memset(hide_q[:], 0.0))
            link(nc.gpsimd.affine_select(out=hide_q[:], in_=hide_q[:], compare_op=ALU.is_ge, fill=BIG,
                                         base=0, pattern=[[1, P]], channel_multiplier=-1))
            link(nc.gpsimd.memset(hide_k[:], 0.0))
            link(nc.gpsimd.affine_select(out=hide_k[:], in_=hide_k[:], compare_op=ALU.is_ge, fill=BIG,
                                         base=0, pattern=[[-1, P]], channel_multiplier=1))
            pool.wait_ge(small_loaded, 16 * (SEC + 2))
            link(nc.gpsimd.affine_select(out=sim_bd[:], in_=sim_bd[:], compare_op=ALU.not_equal, fill=1.0,
                                         base=0, pattern=[[-1, P]], channel_multiplier=1))
            link(nc.gpsimd.memset(v1[:, :, :, D:D + 1], 1.0))
            link(nc.gpsimd.memset(ks[32:64, :].bitcast(f32), 1.0))
            nc.gpsimd.memset(ks[96:128, :].bitcast(f32), 1.0).then_inc(consts_ready, 1)
            for n in range(B):
                rsqrt(n)
            pool.wait_ge(raw_loaded, 16 * 3)
            link(nc.gpsimd.memset(wk_hi[:].bitcast(f32), 0.0))
            link(nc.gpsimd.memset(wk_lo[:].bitcast(f32), 0.0))
            raw = probs[:, 0, 0:KC * C].rearrange("p (k n) -> p k n", k=KC)
            raw_kv = probs[:, 1, 0:2 * KC * D].rearrange("p (k n) -> p k n", k=KC)
            link(nc.gpsimd.tensor_copy(wq_hi[:], raw))
            link(nc.gpsimd.tensor_tensor(wq_lo[:], raw, wq_hi[:].bitcast(f32), ALU.subtract))
            link(nc.gpsimd.tensor_copy(wv_hi[:], raw_kv[:, :, D:2 * D]))
            link(nc.gpsimd.tensor_tensor(wv_lo[:], raw_kv[:, :, D:2 * D], wv_hi[:].bitcast(f32), ALU.subtract))
            for n in (0, 1, 2, 4, 5, 6):
                cols = slice(n * D, (n + 1) * D)
                link(nc.gpsimd.tensor_copy(wk_hi[:, :, cols], raw_kv[:, :, 0:D]))
                last = nc.gpsimd.tensor_tensor(wk_lo[:, :, cols], raw_kv[:, :, 0:D],
                                               wk_hi[:, :, cols].bitcast(f32), ALU.subtract)
                if n == 6:
                    last.then_inc(attn_w_ready, 1)
                else:
                    link(last)
            for n in range(B, 3 * B):
                rsqrt(n)

        @block.scalar
        def _(act):
            def copy(out_, in_, scale=1.0):
                return nc.scalar.activation(out_, in_, ACT.Copy, scale=scale)

            act.dma_start(work[0:E, 0, :], gate_w).then_inc(small_loaded, 16)
            act.dma_start(bo_row[:], bo.rearrange("(a c) -> a c", a=1)).then_inc(small_loaded, 16)
            act.wait_ge(zeros_ready, 1)
            for n in range(SEC):
                act.dma_start(sim_bd[n * E:(n + 1) * E, n * E:(n + 1) * E], sim).then_inc(small_loaded, 16)
            act.dma_start(probs[:, 0, 0:KC * C].rearrange("p (k n) -> p k n", k=KC),
                          wq.rearrange("(k p) n -> p k n", p=P)).then_inc(raw_loaded, 16)
            raw_kv = probs[:, 1, 0:2 * KC * D].rearrange("p (k n) -> p k n", k=KC)
            act.dma_start(raw_kv[:, :, 0:D], wk.rearrange("(k p) n -> p k n", p=P)).then_inc(raw_loaded, 16)
            act.dma_start(raw_kv[:, :, D:2 * D], wv.rearrange("(k p) n -> p k n", p=P)).then_inc(raw_loaded, 16)
            act.dma_start(wo_sb[:], wo.rearrange("(k p) n -> p k n", p=P)).then_inc(wo_loaded, 16)

            def fetch(name, n, k):
                act.wait_ge(filled[k], JOB[name, n, k] + 1)

            def split_weights(g, s, done):
                act.wait_ge(w_transposed, done + 1)
                o, i = prep_out(wgu_hi, wd_hi, g, s)
                copy(o, i).then_inc(w_hi_ready, 1)

            def stage(name, n):
                if name == "PREP":
                    for s in range(STEPS):
                        split_weights(0, s, s)
                elif name == "GW":
                    fetch(name, n, 2)
                    copy(gw_hi[:].rearrange("p k e -> p (k e)"), scr[2][:, 0:KC * E]).then_inc(copied[2], 1)
                elif name == "LN":
                    fetch(name, n, 0)
                    cols = slice(T * (n % B), T * (n % B + 1))
                    copy(xt_hi[:, :, cols], scr[0].rearrange("p (k n) -> p k n", k=KC)).then_inc(copied[0], 1)
                elif name == "R1":
                    act.wait_ge(drained[2], JOB[name, n, 2] + 1)
                    nc.scalar.activation(pr[:], pr[:], ACT.Exp).then_inc(router_exp, 1)
                elif name == "R2":
                    fetch(name, n, 0)
                    if n >= 1:
                        act.wait_ge(filled[1], JOB[name, n - 1, 1] + 1)
                    copy(onehot_t[:], scr[0][:, 0:P].bitcast(bf16).rearrange("p (i n) -> p i n", i=BT)).then_inc(drained[0], 1)
                elif name == "QK":
                    fetch(name, n, 1)
                    if n >= 1:
                        act.wait_ge(q_moved, 16 * MOVES * n)
                    copy(ht_hi[:, :, :].rearrange("p a n -> p (a n)")[:, 0:2 * T], scr[1], scale=D ** -0.5).then_inc(copied[1], 1)
                elif name == "SM":
                    fetch(name, n, 2)
                    if n >= 1:
                        act.wait_ge(max_moved, 16 * n)
                    copy(neg_max_t[:], scr[2][0:H, 0:T]).then_inc(drained[2], 1)
                elif name == "PV":
                    for w in range(HP):
                        for half, (lo, hi) in enumerate(((0, 2 * T), (2 * T, 3 * T))):
                            r = CHUNK[name, n] + 2 * w + half
                            act.wait_ge(ring_filled, r + 1)
                            if half == 0 and HP * n + w >= 2:
                                act.wait_ge(probs_used, HP * n + w - 1)
                            if half == 0 and HP * n + w < 2:
                                act.wait_ge(attn_w_ready, 1)
                            k, _ = ring_use(r)
                            nc.scalar.activation(probs[:, w % 2, lo:hi], ring[k][:, 0:hi - lo], ACT.Exp)\
                                .then_inc(ring_drained[k], 1)
                elif name == "OU":
                    fetch(name, n, 0)
                    if n >= 1:
                        act.wait_ge(filled[1], JOB[name, n - 1, 1] + 1)
                    copy(at[:], scr[0].rearrange("p (i n) -> p i n", i=BT)).then_inc(drained[0], 1)

            def unit(u, t):
                act.wait_ge(gu_done, u + 1)
                if not (isinstance(u, int) and u < 2):
                    act.wait_ge(tr_done, u - 1)
                gate = pair[t % 2][:, :, 0:HC].rearrange("p a (e n) -> p a e n", e=2)[:, :, :, 0:F]
                nc.scalar.activation(h[:, t % 2].rearrange("p (a e) n -> p a e n", a=2), gate, ACT.Silu).then_inc(silu_done, 1)

            def keep_hi(u, t):
                act.wait_ge(tr_done, u + 1)
                if not (isinstance(u, int) and u < 2):
                    act.wait_ge(dn_done, u - 1)
                copy(ht_hi[:, t % 2, :], scr[t % 2][:, 0:FC * P]).then_inc(ht_hi_ready, 1)

            def group(g, u0, prepare, first):
                for t in range(NT):
                    unit(u0 + t, t)
                    if not (first and t == 0):
                        keep_hi(u0 + (t - 1), t - 1)
                    if prepare and t < STEPS:
                        split_weights(g + 1, t, g * STEPS + STEPS + t)

            def moe_pass(p):
                group(0, p * UNITS, p == 0, True)
                with act.Fori(1, G - 1) as g:
                    group(g, g * NT + p * UNITS, p == 0, False)
                group(G - 1, (G - 1) * NT + p * UNITS, False, False)
                keep_hi((p + 1) * UNITS - 1, NT - 1)

            for name, n in PROLOGUE:
                stage(name, n)
            moe_pass(0)
            for name, n in ATTENTION:
                stage(name, n)
            moe_pass(1)

        @block.vector
        def _(dve):
            steps = [0]

            def link(ins):
                steps[0] += 1
                ins.then_inc(dve_chain, 1)
                dve.wait_ge(dve_chain, steps[0])

            V = nc.vector

            def fetch(name, n, k):
                dve.wait_ge(filled[k], JOB[name, n, k] + 1)

            def split_weights(g, s, done):
                dve.wait_ge(w_hi_ready, done + 1)
                o, i = prep_out(wgu_lo, wd_lo, g, s)
                o_hi, _ = prep_out(wgu_hi, wd_hi, g, s)
                V.tensor_tensor(o, i, o_hi.bitcast(f32), ALU.subtract).then_inc(w_ready, 1)

            def layernorm(n):
                b = n % B
                if n < B:
                    dve.wait_ge(x_loaded[b], 16)
                for i in range(BT):
                    link(V.bn_stats(stats[:, i, :], x[:, BT * b + i, :]))
                for i in range(BT):
                    link(V.bn_aggr(mv[:, i, :], stats[:, i, :]))
                V.tensor_scalar(var_eps[:], mv[:, :, 1], EPS, None, ALU.add).then_inc(var_ready, 1)
                dve.wait_ge(rstd_ready, SEQ["LN", n] + 1)
                if n == 0:
                    dve.wait_ge(filled[2], JOB["GW", 0, 2] + 1)
                for i in range(BT):
                    ins = V.tensor_scalar(work[:, i, :], x[:, BT * b + i, :], mv[:, i, 0:1], rstd[:, i:i + 1],
                                          ALU.subtract, ALU.mult)
                ins.then_inc(xn_ready, 1)
                dve.wait_ge(copied[0], SEQ["LN", n] + 1)
                cols = slice(T * b, T * (b + 1))
                V.tensor_tensor(xt_lo[:, :, cols], scr[0].rearrange("p (k n) -> p k n", k=KC),
                                xt_hi[:, :, cols].bitcast(f32), ALU.subtract).then_inc(drained[0], 1)
                dve.wait_ge(drained[0], JOB["LN", n, 0] + 1)

            def router_top(n):
                fetch("R1", n, 2)
                logits = scr[2][:, 0:BT * E].rearrange("p (i e) -> p i e", i=BT)
                oh = onehot[:, n % 2]
                link(V.tensor_reduce(pmax[:], logits, AX, ALU.max))
                V.tensor_tensor(pr[:], logits, pmax[:, :, None].to_broadcast([P, BT, E]), ALU.subtract)\
                    .then_inc(drained[2], 1)
                dve.wait_ge(router_exp, n + 1)
                link(V.tensor_reduce(psumm[:], pr[:], AX, ALU.add))
                link(V.reciprocal(psumm[:], psumm[:]))
                link(V.tensor_tensor(pr[:], pr[:], psumm[:, :, None].to_broadcast([P, BT, E]), ALU.mult))
                w8 = top[:, n % 2]
                for i in range(BT):
                    link(V.max(w8[:, i, :], pr[:, i, :]))
                for i in range(BT):
                    link(V.max_index(top_i[:, i, :], w8[:, i, :], pr[:, i, :]))
                link(V.tensor_copy(top_f[:], top_i[:]))
                if n == 0:
                    dve.wait_ge(consts_ready, 1)
                if n >= 2:
                    dve.wait_ge(filled[0], JOB["R2", n - 2, 0] + 1)
                for i in range(BT):
                    ins = V.tensor_tensor(oh[:, i], top_f[:, i, :, None].to_broadcast([P, TOP, E]),
                                          iota[:, None, :].to_broadcast([P, TOP, E]), ALU.is_equal)
                ins.then_inc(onehot_ready, 1)
                dve.wait_ge(onehot_ready, n + 1)
                link(V.tensor_reduce(psumm[:], w8, AX, ALU.add))
                link(V.tensor_scalar(psumm[:], psumm[:], 1e-12, None, ALU.max))
                link(V.reciprocal(psumm[:], psumm[:]))
                link(V.tensor_tensor(w8, w8, psumm[:, :, None].to_broadcast([P, BT, TOP]), ALU.mult))

            def router_combine(n):
                b, oh, w8 = n % B, onehot[:, n % 2], top[:, n % 2]
                prod = work[:, :, :].rearrange("p i c -> p (i c)")
                prod4 = prod.rearrange("p (j k e) -> p j k e", j=SEC, k=PRIM)
                fetch("R2", n, 1)
                dve.wait_ge(onehot_ready, n + 1)
                for i in range(BT):
                    rows = scr[1][:, i * P:(i + 1) * P].rearrange("p (j e) -> p j e", j=SEC)
                    ins = V.tensor_tensor(prod4, rows[:, :, None, :].to_broadcast([P, SEC, PRIM, E]),
                                          oh[:, i, None, 0:PRIM, :].to_broadcast([P, SEC, PRIM, E]), ALU.mult)
                    if i == BT - 1:
                        ins.then_inc(drained[1], 1)
                        dve.wait_ge(drained[1], JOB["R2", n, 1] + 1)
                    else:
                        link(ins)
                    link(V.tensor_reduce(cand[:, i], prod4, AX, ALU.add))
                four = [P, BT, SEC, PRIM]
                link(V.tensor_reduce(best[:], cand[:], AX, ALU.max))
                for i in range(BT):
                    link(V.tensor_tensor(pick[:, i], cand[:, i], best[:, i, :, None].to_broadcast(four[0:1] + four[2:]), ALU.is_equal))
                    link(V.tensor_tensor(pick[:, i], pick[:, i], rank[:, None, :].to_broadcast(four[0:1] + four[2:]), ALU.mult))
                link(V.tensor_reduce(moved[:], pick[:], AX, ALU.max))
                for i in range(BT):
                    link(V.tensor_tensor(pick[:, i], pick[:, i], moved[:, i, :, None].to_broadcast(four[0:1] + four[2:]), ALU.is_equal))
                link(V.tensor_scalar(best[:], best[:], 0.5, None, ALU.is_ge))
                link(V.tensor_tensor(moved[:], best[:], w8[:, :, PRIM:TOP], ALU.mult))
                for i in range(BT):
                    link(V.tensor_tensor(pick[:, i], pick[:, i], moved[:, i, :, None].to_broadcast(four[0:1] + four[2:]), ALU.mult))
                link(V.tensor_reduce(gain[:], pick[:].rearrange("p i j k -> p i k j"), AX, ALU.add))
                link(V.tensor_tensor(slot_w[:, :, 0:PRIM], w8[:, :, 0:PRIM], gain[:], ALU.add))
                link(V.tensor_tensor(slot_w[:, :, PRIM:TOP], w8[:, :, PRIM:TOP], moved[:], ALU.subtract))
                prod8 = prod.rearrange("p (i k e) -> p i k e", i=BT, k=TOP)
                for i in range(BT):
                    link(V.tensor_tensor(prod8[:, i], oh[:, i], slot_w[:, i, :, None].to_broadcast([P, TOP, E]), ALU.mult))
                V.tensor_reduce(cw[:, BT * b:BT * (b + 1), :], prod8.rearrange("p i k e -> p i e k"), AX, ALU.add)\
                    .then_inc(cw_ready, 1)
                dve.wait_ge(cw_ready, n + 1)

            def stage(name, n):
                if name == "PREP":
                    for s in range(STEPS):
                        split_weights(0, s, s)
                elif name == "GW":
                    dve.wait_ge(copied[2], 1)
                    V.tensor_tensor(gw_lo[:].rearrange("p k e -> p (k e)"), scr[2][:, 0:KC * E],
                                    gw_hi[:].rearrange("p k e -> p (k e)").bitcast(f32), ALU.subtract).then_inc(drained[2], 1)
                elif name == "LN":
                    layernorm(n)
                elif name == "R1":
                    router_top(n)
                elif name == "R2":
                    router_combine(n)
                elif name == "QK":
                    dve.wait_ge(copied[1], n + 1)
                    flat_hi = ht_hi[:, :, :].rearrange("p a n -> p (a n)")[:, 0:2 * T]
                    flat_lo = ht_lo[:, :, :].rearrange("p a n -> p (a n)")[:, 0:2 * T]
                    V.scalar_tensor_tensor(flat_lo, scr[1], D ** -0.5, flat_hi.bitcast(f32), ALU.mult, ALU.subtract)\
                        .then_inc(drained[1], 1)
                    fetch(name, n, 2)
                    if n == 0:
                        dve.wait_ge(consts_ready, 1)
                    if n >= 2:
                        dve.wait_ge(probs_used, HP * (n - 1))
                    o = base(n)
                    link(V.tensor_copy(ks[o:o + 3 * D, :], scr[2][o:o + 3 * D, 0:T]))
                    low = slice(o + 2 * D, o + 3 * D)
                    link(V.tensor_tensor(ks[low, :], scr[2][low, 0:T], ks[low, :].bitcast(f32), ALU.subtract))
                    V.tensor_copy(v1[:, n % 2, :, 0:D], scr[2][:, T:T + BT * D].rearrange("p (i d) -> p i d", i=BT))\
                        .then_inc(drained[2], 1)
                elif name == "SM":
                    r = CHUNK[name, n]
                    for i, (heads, width) in enumerate(((4, P), (2, T))):
                        for hh in range(0, H, heads):
                            dve.wait_ge(ring_filled, r + 1)
                            k, _ = ring_use(r)
                            V.tensor_reduce(neg_max[:, i, hh:hh + heads], ring[k].rearrange("p (a n) -> p a n", a=heads),
                                            AX, ALU.max, negate=True).then_inc(ring_drained[k], 1)
                            r += 1
                elif name == "OU":
                    dve.wait_ge(probs_used, HP * (n + 1))
                    for i in range(BT):
                        link(V.reciprocal(rsum[:, i, :], pv[i].rearrange("p (h d) -> p h d", h=H)[:, :, D]))
                    for i in range(BT):
                        ins = V.tensor_tensor(work[:, i, :].rearrange("p (h d) -> p h d", h=H),
                                              pv[i].rearrange("p (h d) -> p h d", h=H)[:, :, 0:D],
                                              rsum[:, i, :, None].to_broadcast([P, H, D]), ALU.mult)
                    ins.then_inc(attn_ready, 1)
                    fetch(name, n, 1)
                    tiles = slice(BT * n, BT * (n + 1))
                    V.tensor_tensor(x[:, tiles, :], scr[1].rearrange("p (i c) -> p i c", i=BT), x[:, tiles, :], ALU.add)\
                        .then_inc(drained[1], 1)
                    dve.wait_ge(drained[1], JOB[name, n, 1] + 1)

            def weigh(g, u, t, p):
                if isinstance(g, int) and g == 0:
                    dve.wait_ge(cw_ready, B * p + t // BT + 1)
                dve.wait_ge(silu_done, u + 1)
                up = pair[t % 2][:, :, 0:HC].rearrange("p a (e n) -> p a e n", e=2)[:, :, :, F:2 * F]
                for e in range(EG):
                    ins = V.scalar_tensor_tensor(h[:, t % 2, e, :], h[:, t % 2, e, :], cw[:, t, bass.ds(g * EG + e, 1)],
                                                 up[:, e // 2, e % 2, :], ALU.mult, ALU.mult)
                ins.then_inc(h_ready, 1)

            def keep_lo(u, t):
                dve.wait_ge(ht_hi_ready, u + 1)
                if not (isinstance(u, int) and u < 2):
                    dve.wait_ge(dn_done, u - 1)
                V.tensor_tensor(ht_lo[:, t % 2, :], scr[t % 2][:, 0:FC * P], ht_hi[:, t % 2, :].bitcast(f32),
                                ALU.subtract).then_inc(ht_ready, 1)

            def add(u, t):
                dve.wait_ge(dn_done, u + 1)
                if not (isinstance(u, int) and u < 3):
                    dve.wait_ge(x_added, u - 2)
                V.scalar_tensor_tensor(x[:, t, :], scr[2][:, 0:C], 0.5, x[:, t, :], ALU.mult, ALU.add).then_inc(x_added, 1)

            def group(g, u0, prepare, first, p):
                for t in range(NT):
                    weigh(g, u0 + t, t, p)
                    if not (first and t < 1):
                        keep_lo(u0 + (t - 1), (t - 1) % NT)
                    if not (first and t < 2):
                        add(u0 + (t - 2), (t - 2) % NT)
                    if prepare and t < STEPS:
                        split_weights(g + 1, t, g * STEPS + STEPS + t)

            def moe_pass(p):
                group(0, p * UNITS, p == 0, True, p)
                with dve.Fori(1, G - 1) as g:
                    group(g, g * NT + p * UNITS, p == 0, False, p)
                group(G - 1, (G - 1) * NT + p * UNITS, False, False, p)
                end = (p + 1) * UNITS
                keep_lo(end - 1, NT - 1)
                add(end - 2, NT - 2)
                add(end - 1, NT - 1)
                dve.wait_ge(x_added, end)

            for name, n in PROLOGUE:
                stage(name, n)
            moe_pass(0)
            for name, n in ATTENTION:
                stage(name, n)
            moe_pass(1)

        @block.tensor
        def _(pe):
            def mm(out_, lhs, rhs, start, stop, **kw):
                return nc.tensor.matmul(out_, lhs, rhs, start=start, stop=stop, **kw)

            def claim(name, n, k):
                if JOB[name, n, k] > 0:
                    pe.wait_ge(drained[k], JOB[name, n, k])

            def claim_ring(r):
                k, before = ring_use(r)
                if before > 0:
                    pe.wait_ge(ring_drained[k], before)
                return ring[k]

            def prepare_weights(s, done):
                if s == 0:
                    pe.wait_ge(gu_loaded, (done // STEPS + 1) * 16 if isinstance(done, int) else done_loads(done, 16))
                if s == RB // 2:
                    pe.wait_ge(d_loaded, (done // STEPS + 1) * 32 if isinstance(done, int) else done_loads(done, 32))
                if not (isinstance(done, int) and done == 0):
                    pe.wait_ge(w_ready, done)
                for raw, col in prep_parts(s):
                    ins = nc.tensor.transpose(prep[:, col:col + P], raw, ident[:])
                ins.then_inc(w_transposed, 1)

            loads = {}

            def done_loads(done, each):
                return loads["groups"] * each

            def stage(name, n):
                b = n % B
                cols = slice(T * b, T * (b + 1))
                if name == "PREP":
                    for s in range(STEPS):
                        prepare_weights(s, s)
                elif name == "GW":
                    pe.wait_ge(small_loaded, 16 * (SEC + 2))
                    pe.wait_ge(consts_ready, 1)
                    for k in range(KC):
                        ins = nc.tensor.transpose(scr[2][:, k * E:(k + 1) * E], work[0:E, 0, k * P:(k + 1) * P], ident[0:E, 0:E])
                    ins.then_inc(filled[2], 1)
                elif name == "LN":
                    claim(name, n, 0)
                    pe.wait_ge(xn_ready, SEQ[name, n] + 1)
                    for k in range(KC):
                        for i in range(BT):
                            ins = nc.tensor.transpose(scr[0][:, (k * BT + i) * P:(k * BT + i + 1) * P],
                                                      work[:, i, k * P:(k + 1) * P], ident[:])
                    ins.then_inc(filled[0], 1)
                elif name == "R1":
                    claim(name, n, 2)
                    pe.wait_ge(drained[0], JOB["LN", n if n < B else n + B, 0] + 1)
                    for i in range(BT):
                        tok = slice(T * b + i * P, T * b + (i + 1) * P)
                        parts = [(a, w, k) for k in range(KC) for a, w in
                                 ((xt_lo, gw_lo), (xt_hi, gw_lo), (xt_lo, gw_hi), (xt_hi, gw_hi))]
                        for m, (a, w, k) in enumerate(parts):
                            ins = mm(scr[2][:, i * E:(i + 1) * E], a[:, k, tok], w[:, k, :], m == 0, m == len(parts) - 1)
                    ins.then_inc(filled[2], 1)
                elif name == "R2":
                    claim(name, n, 0)
                    pe.wait_ge(onehot_ready, n + 1)
                    flipped = scr[0][:, 0:P].bitcast(bf16)
                    for i in range(BT):
                        ins = nc.tensor.transpose(flipped[:, i * P:(i + 1) * P],
                                                  onehot[:, n % 2, i, PRIM:TOP, :].rearrange("p k e -> p (k e)"),
                                                  ident_b[:, P:2 * P])
                    ins.then_inc(filled[0], 1)
                    claim(name, n, 1)
                    pe.wait_ge(drained[0], JOB[name, n, 0] + 1)
                    for i in range(BT):
                        ins = mm(scr[1][:, i * P:(i + 1) * P], onehot_t[:, i, :], sim_bd[:], True, True)
                    ins.then_inc(filled[1], 1)
                elif name == "QK":
                    claim(name, n, 1)
                    pe.wait_ge(drained[0], JOB["LN", B + n, 0] + 1)
                    if n == 0:
                        pe.wait_ge(attn_w_ready, 1)
                    for blk in range(H // HB):
                        parts = [(w, a, k) for k in range(KC) for w, a in ((wq_hi, xt_lo), (wq_lo, xt_hi), (wq_hi, xt_hi))]
                        for m, (w, a, k) in enumerate(parts):
                            ins = mm(scr[1][:, blk * T:(blk + 1) * T], w[:, k, blk * P:(blk + 1) * P], a[:, k, cols],
                                     m == 0, m == len(parts) - 1)
                    ins.then_inc(filled[1], 1)
                    claim(name, n, 2)
                    parts = [(w, a, k) for k in range(KC) for w, a in ((wk_hi, xt_lo), (wk_lo, xt_hi), (wk_hi, xt_hi))]
                    for m, (w, a, k) in enumerate(parts):
                        mm(scr[2][0:7 * D, 0:T], w[:, k, :], a[:, k, cols], m == 0, m == len(parts) - 1)
                    for i in range(BT):
                        tok = slice(T * b + i * P, T * b + (i + 1) * P)
                        parts = [(a, w, k) for k in range(KC) for a, w in
                                 ((xt_hi, wv_lo), (xt_lo, wv_hi), (xt_hi, wv_hi))]
                        for m, (a, w, k) in enumerate(parts):
                            ins = mm(scr[2][:, T + i * D:T + (i + 1) * D], a[:, k, tok], w[:, k, :], m == 0, m == len(parts) - 1)
                    ins.then_inc(filled[2], 1)
                elif name == "SM":
                    pe.wait_ge(q_moved, 16 * MOVES * (n + 1))
                    pe.wait_ge(drained[2], JOB["QK", n, 2] + 1)
                    o = base(n)
                    rows = slice(o, o + 3 * D)
                    r = CHUNK[name, n]
                    for i, (heads, width) in enumerate(((4, P), (2, T))):
                        mask = ident_b[:, 2 * P - width:2 * P]
                        for hh in range(0, H, heads):
                            dst = claim_ring(r)
                            mm(dst, hide_q[:], mask[:, None, :].to_broadcast([P, heads, width]), True, False,
                               skip_group_check=True)
                            for a in range(heads):
                                ins = mm(dst[:, a * width:(a + 1) * width], qs[rows, hh + a, i * P:(i + 1) * P],
                                         ks[rows, 0:width], False, a == heads - 1, skip_group_check=True)
                            ins.then_inc(ring_filled, 1)
                            r += 1
                    claim(name, n, 2)
                    for k in range(RING):
                        pe.wait_ge(ring_drained[k], ring_use_count(r, k))
                    for i in range(BT):
                        ins = nc.tensor.transpose(scr[2][0:H, i * P:(i + 1) * P], neg_max[:, i, :], ident[:])
                    ins.then_inc(filled[2], 1)
                elif name == "PV":
                    pe.wait_ge(max_moved, 16 * (n + 1))
                    o = base(n)
                    rows = slice(o, o + 3 * D + 1)
                    for w in range(HP + 1):
                        if w < HP:
                            r = CHUNK[name, n] + 2 * w
                            heads = slice(2 * w, 2 * w + 2)
                            dst = claim_ring(r)
                            for_mask = ident_b[:, P:2 * P]
                            mm(dst.rearrange("p (a n) -> p a n", a=2)[:, :, 0:P], hide_k[:],
                               for_mask[:, None, :].to_broadcast([P, 2, P]), True, False, skip_group_check=True)
                            mm(dst.rearrange("p (a n) -> p a n", a=2), ks[rows, 0:P], qs[rows, heads, :],
                               False, True, skip_group_check=True).then_inc(ring_filled, 1)
                            dst = claim_ring(r + 1)[:, 0:2 * P]
                            mm(dst.rearrange("p (a n) -> p a n", a=2), hide_k[:],
                               for_mask[:, None, :].to_broadcast([P, 2, P]), True, False, skip_group_check=True)
                            mm(dst.rearrange("p (a n) -> p a n", a=2), ks[rows, P:T], qs[rows, heads, P:T],
                               False, True, skip_group_check=True).then_inc(ring_filled, 1)
                        if w >= 1:
                            times_v(n, w - 1)
                elif name == "OU":
                    claim(name, n, 0)
                    pe.wait_ge(attn_ready, n + 1)
                    for i in range(BT):
                        for k in range(KC):
                            ins = nc.tensor.transpose(scr[0][:, (i * KC + k) * P:(i * KC + k + 1) * P],
                                                      work[:, i, k * P:(k + 1) * P], ident[:])
                    ins.then_inc(filled[0], 1)
                    claim(name, n, 1)
                    if n == 0:
                        pe.wait_ge(wo_loaded, 16)
                    pe.wait_ge(drained[0], JOB[name, n, 0] + 1)
                    for i in range(BT):
                        dst = scr[1][:, i * C:(i + 1) * C]
                        mm(dst, ones_row[0:1, :], bo_row[0:1, :], True, False)
                        for k in range(KC):
                            ins = mm(dst, at[:, i, k * P:(k + 1) * P], wo_sb[:, k, :], False, k == KC - 1)
                    ins.then_inc(filled[1], 1)

            def times_v(n, w):
                for half in range(2):
                    k, before = ring_use(CHUNK["PV", n] + 2 * w + half)
                    pe.wait_ge(ring_drained[k], before + 1)
                if w == 0 and n >= 1:
                    pe.wait_ge(attn_ready, n)
                for a in range(2):
                    dst = slice((2 * w + a) * (D + 1), (2 * w + a + 1) * (D + 1))
                    mm(pv[0][:, dst], probs[:, w % 2, a * T:a * T + P], v1[:, n % 2, 0, :], True, True)
                    mm(pv[1][:, dst], probs[:, w % 2, a * T + P:(a + 1) * T], v1[:, n % 2, 0, :], True, False)
                    ins = mm(pv[1][:, dst], probs[:, w % 2, 2 * T + a * P:2 * T + (a + 1) * P], v1[:, n % 2, 1, :], False, True)
                ins.then_inc(probs_used, 1)

            def gate_up_products(g, u, t, p):
                if not (isinstance(u, int) and u < 2):
                    pe.wait_ge(h_ready, u - 1)
                if isinstance(g, int) and g == 0:
                    pe.wait_ge(drained[0], JOB["LN", 2 * B * p + t // BT, 0] + 1)
                tok = slice(t * P, (t + 1) * P)
                for a in range(2):
                    parts = [(x_, w, k) for k in range(KC) for x_, w in ((xt_hi, wgu_lo), (xt_hi, wgu_hi), (xt_lo, wgu_hi))]
                    for m, (x_, w, k) in enumerate(parts):
                        ins = mm(pair[t % 2][:, a, 0:HC], x_[:, k, tok], w[:, g, k, a * HC:(a + 1) * HC],
                                 m == 0, m == len(parts) - 1)
                ins.then_inc(gu_done, 1)

            def transpose_h(u, t):
                pe.wait_ge(h_ready, u + 1)
                if not (isinstance(u, int) and u < 2):
                    pe.wait_ge(ht_ready, u - 1)
                flat = h[:, t % 2].rearrange("p e f -> p (e f)")
                for j in range(FC):
                    ins = nc.tensor.transpose(scr[t % 2][:, j * P:(j + 1) * P], flat[:, j * P:(j + 1) * P], ident[:])
                ins.then_inc(tr_done, 1)

            def down_products(g, u, t):
                pe.wait_ge(ht_ready, u + 1)
                if not (isinstance(u, int) and u < 1):
                    pe.wait_ge(x_added, u)
                parts = [(a, w, j) for j in range(FC) for a, w in ((ht_hi, wd_lo), (ht_hi, wd_hi), (ht_lo, wd_hi))]
                for m, (a, w, j) in enumerate(parts):
                    ins = mm(scr[2][:, 0:C], a[:, t % 2, j * P:(j + 1) * P], w[:, g, j, :], m == 0, m == len(parts) - 1)
                ins.then_inc(dn_done, 1)

            def group(g, u0, prepare, first, p):
                if p == 0:
                    pe.wait_ge(w_ready, g * STEPS + STEPS)
                for t in range(NT):
                    gate_up_products(g, u0 + t, t, p)
                    if not (first and t < 1):
                        transpose_h(u0 + (t - 1), (t - 1) % NT)
                    if not (first and t < 2):
                        down_products(g - 1 if t < 2 else g, u0 + (t - 2), (t - 2) % NT)
                    if prepare and t < STEPS:
                        loads["groups"] = g + 2
                        prepare_weights(t, g * STEPS + STEPS + t)

            def moe_pass(p):
                group(0, p * UNITS, p == 0, True, p)
                with pe.Fori(1, G - 1) as g:
                    group(g, g * NT + p * UNITS, p == 0, False, p)
                group(G - 1, (G - 1) * NT + p * UNITS, False, False, p)
                end = (p + 1) * UNITS
                transpose_h(end - 1, NT - 1)
                down_products(G - 1, end - 2, NT - 2)
                down_products(G - 1, end - 1, NT - 1)

            def scratch_free(jobs):
                for k in range(3):
                    pe.wait_ge(drained[k], jobs[k])

            for name, n in PROLOGUE:
                stage(name, n)
            scratch_free(jobs_at(PROLOGUE))
            moe_pass(0)
            pe.wait_ge(x_added, UNITS)
            for name, n in ATTENTION:
                stage(name, n)
            scratch_free(JOBS)
            moe_pass(1)


def jobs_at(stages):
    return [sum(k in SCRATCH.get(name, ()) for name, _ in stages) for k in range(3)]


def ring_use_count(r, k):
    return len([c for c in range(r) if c % RING == k])


_INS = ["L0_attn_x", "L0_attn_Wq", "L0_attn_Wk", "L0_attn_Wv", "L0_attn_Wo", "L0_attn_bo",
        "L0_ffn_gate_weight", "L0_ffn_gate_up_proj", "L0_ffn_down_proj", "L0_ffn_similarity"]


def kernel(**inputs):
    import numpy as _np
    import concourse.bacc as _bacc
    from concourse import mybir as _mybir
    from concourse.bass_utils import run_bass_kernel_spmd as _run

    nc = _bacc.Bacc("TRN2", target_bir_lowering=False, num_devices=1, dynamic_dma_scratch_size=1024)
    arrays, args = {}, []
    for name in _INS:
        a = _np.ascontiguousarray(inputs[name])
        arrays[f"in_{name}"] = a
        args.append(nc.dram_tensor(f"in_{name}", a.shape, _mybir.dt.from_np(a.dtype), kind="ExternalInput").ap())
    args.append(nc.dram_tensor("out_x", (B, T, C), _mybir.dt.float32, kind="ExternalOutput").ap())
    macaron(nc, *args)
    r = _run(nc, [arrays], core_ids=[0])
    return r.results[0]["out_x"]
```

```python
import concourse.bass as bass
from concourse import mybir
from contextlib import ExitStack

P = 128
B, T, C = 4, 256, 256
NT = B * T // P
BT = T // P
KC = C // P
E, F = 32, 96
TOP, PRIM = 8, 4
SEC = TOP - PRIM
H, D = 16, 16
HB = P // D
EG = 4
G = E // EG
GC = EG * 2 * F
HC = GC // 2
FC = EG * F // P
RB = GC // P
STEPS = RB // 2 + FC
BIG = -1.0e30
EPS = 1e-5
HP = H // 2
MOVES = 3 * (H // HB)
PHASE = G * BT
ALL = 2 * B * PHASE
GU_BANKS = 3

JOBS_OF = {"GW": 1, "LNc": 1, "R1a": 1, "R2a": 1, "R2b": 1, "QK": 2, "SM0": 3, "SM1": 3, "SM2": 3, "SM3": 3,
           "SMT": 1, "OU1": 1, "OU2": 1, "PREP": 1} | {f"PV{w}": 2 for w in range(HP)}
SPLIT = ("GW", "LNc", "QK", "PREP")

LN_R = (("LNa", 0), ("LNb", 1), ("LNc", 2), ("R1a", 3), ("R1b", 4), ("R1c", 5), ("R2a", 6), ("R2b", 7),
        ("R2c", 8), ("R2d", 9))
ATTEND = ((("LNa", 2), ("LNb", 3), ("LNc", 4), ("QK", 5), ("SM0", 7), ("SM1", 8), ("SM2", 9), ("SM3", 10), ("SMT", 11))
          + tuple((f"PV{w}", 13 + w) for w in range(5)) + (("OUn0", 17),)
          + tuple((f"PV{w}", 13 + w) for w in range(5, HP + 1)) + (("OUn1", 13 + HP), ("OU1", 16 + HP), ("OU2", 17 + HP)))
FIRST_ROUTER = {1: 1, 2: 10, 3: 23}


def make_schedule():
    before = [("GW", 0)] + [(name, 0) for name, _ in LN_R[:3]] + [("PREP", s) for s in range(STEPS)]
    before += [(name, 0) for name, _ in LN_R[3:]]
    after = {}
    for b, at in FIRST_ROUTER.items():
        for name, off in LN_R:
            after.setdefault(at + off, []).append((name, b))
    for b in range(B):
        start = PHASE * (b + 1)
        for name, off in ATTEND:
            after.setdefault(start + off, []).append((name, b + (B if name[0] == "L" else 0)))
        for name, off in LN_R:
            after.setdefault(start + 18 + HP + off, []).append((name, b + (2 * B if name[0] == "L" else B)))
    for s in range(STEPS, STEPS * G):
        after.setdefault((s - STEPS) // (STEPS // BT), []).append(("PREP", s))
    return before, after


BEFORE, AFTER = make_schedule()
LAST_STEP = max(AFTER)
ORDER = BEFORE + [step for slot in sorted(AFTER) for step in AFTER[slot]]


def number_jobs():
    job, copy, seq, jobs, copies, seen = {}, {}, {}, 0, 0, {}
    for step in ORDER:
        for i in range(JOBS_OF.get(step[0], 0)):
            job[step, i] = jobs
            jobs += 1
        if step[0] in SPLIT:
            copy[step] = copies
            copies += 1
        seq[step] = seen.get(step[0], 0)
        seen[step[0]] = seq[step] + 1
    return job, copy, seq


JOB, COPY, SEQ = number_jobs()


def phase_of(u):
    return u // PHASE % B, u % PHASE // BT, u % BT


def macaron(nc, x_in, wq, wk, wv, wo, bo, gate_w, gate_up, down, sim, out):
    f32, f32r, bf16, u32 = mybir.dt.float32, mybir.dt.float32r, mybir.dt.bfloat16, mybir.dt.uint32
    ALU, ACT, AX = mybir.AluOpType, mybir.ActivationFunctionType, mybir.AxisListType.X

    x_rows = x_in.rearrange("b (i p) c -> p (b i) c", p=P)
    out_rows = out.rearrange("b (i p) c -> p (b i) c", p=P)
    gate_up_rows = gate_up.rearrange("(g e) f c -> g (e f) c", g=G).rearrange("g (r p) c -> g p r c", p=P)
    down_rows = down.rearrange("(g e) (h p) f -> g h p e f", g=G, p=P)
    q_dram = nc.dram_tensor("q_dram", (B, 2, P, H // HB, T), f32, kind="Internal").ap()

    with ExitStack() as ctx:
        def sb(name, shape, dt, stack=ctx):
            return stack.enter_context(nc.sbuf_tensor(name, shape, dt))

        def sem(name):
            return ctx.enter_context(nc.semaphore(name))

        x = sb("x", [P, NT, C], f32)
        xt_hi = sb("xt_hi", [P, KC, B * T], f32r)
        xt_lo = sb("xt_lo", [P, KC, B * T], f32r)
        wgu_hi = sb("wgu_hi", [P, G, KC, GC], f32r)
        wgu_lo = sb("wgu_lo", [P, G, KC, GC], f32r)
        wd_hi = sb("wd_hi", [P, G, FC, C], f32r)
        wd_lo = sb("wd_lo", [P, G, FC, C], f32r)
        h = sb("h", [P, 2, EG, F], f32)
        ht_hi = sb("ht_hi", [P, 2, FC * P], f32r)
        ht_lo = sb("ht_lo", [P, 2, FC * P], f32r)
        cw = sb("cw", [P, NT, E], f32)
        with ExitStack() as first_phase:
            raw_gu = sb("raw_gu", [P, RB, C], f32, first_phase)
            raw_d = sb("raw_d", [P, KC, EG, F], f32, first_phase)
        qs = sb("qs", [P, H, T], f32r)
        probs = sb("probs", [P, 2, 3 * T], f32)
        work = sb("work", [P, 2, 2 * T], f32)
        xn = work[:, 0, :].rearrange("p (i c) -> p i c", i=BT)
        attn_t, prod = xn, work[:, 0, :]
        q_hi, q_lo = work[:, 0, :].bitcast(f32r), work[:, 1, :].bitcast(f32r)
        wq_hi, wq_lo = sb("wq_hi", [P, KC, C], f32r), sb("wq_lo", [P, KC, C], f32r)
        wk_hi, wk_lo = sb("wk_hi", [P, KC, 7 * D], f32r), sb("wk_lo", [P, KC, 7 * D], f32r)
        wv_hi, wv_lo = sb("wv_hi", [P, KC, D], f32r), sb("wv_lo", [P, KC, D], f32r)
        wo_sb = sb("wo_sb", [P, KC, C], f32)
        rows_ = sb("rows_", [33, C + P], f32)
        neg_max_t = rows_[0:H, 0:T]
        bo_row, ones_row = rows_[32:33, 0:C], rows_[32:33, C:C + P]
        ks = sb("ks", [P, T], f32r)
        v1 = sb("v1", [P, 2, BT, D + 1], f32)
        neg_max = sb("neg_max", [P, BT, H], f32)
        attn = sb("attn", [P, BT, C], f32)
        rsum = sb("rsum", [P, BT, HB], f32)
        ident = sb("ident", [P, P], f32)
        ident_b = sb("ident_b", [P, P], bf16)
        hide_q = sb("hide_q", [P, P], bf16)
        hide_k = sb("hide_k", [P, P], bf16)
        iota = sb("iota", [P, E], f32)
        rank = sb("rank", [P, PRIM], f32)
        minus_half = sb("minus_half", [P, BT], f32)
        stats, mv = sb("stats", [P, BT, 6], f32), sb("mv", [P, BT, 2], f32)
        var_eps, rstd = sb("var_eps", [P, BT], f32), sb("rstd", [P, BT], f32)
        gw_hi, gw_lo = sb("gw_hi", [P, KC, E], f32r), sb("gw_lo", [P, KC, E], f32r)
        sim_bd = sb("sim_bd", [P, P], f32)
        pr = sb("pr", [P, BT, E], f32)
        pmax, total = sb("pmax", [P, BT], f32), sb("total", [P, BT], f32)
        top = sb("top", [P, BT, TOP], f32)
        top_i, top_f = sb("top_i", [P, BT, TOP], u32), sb("top_f", [P, BT, TOP], f32)
        onehot = sb("onehot", [P, BT, TOP, E], bf16)
        onehot_t = sb("onehot_t", [P, BT, P], f32)
        cand = sb("cand", [P, BT, SEC, PRIM], f32)
        pick = sb("pick", [P, BT, SEC, PRIM], f32)
        best, moved = sb("best", [P, BT, SEC], f32), sb("moved", [P, BT, SEC], f32)
        gain, slot_w = sb("gain", [P, BT, PRIM], f32), sb("slot_w", [P, BT, TOP], f32)

        def bank(name):
            return ctx.enter_context(nc.psum_tensor(name, [P, 512], f32))
        gu_banks = [bank(f"gu{i}") for i in range(GU_BANKS)]
        tr_bank, dn_bank, pv_bank = bank("tr"), bank("dn"), bank("pv")
        job_banks = [bank("job0"), bank("job1")]
        gu_banks.append(job_banks[0])
        pv = pv_bank[:, 0:BT * HB * (D + 1)].rearrange("p (i h d) -> p i h d", i=BT, h=HB)

        x_loaded = [sem(f"x_loaded{b}") for b in range(B)]
        small_loaded, raw_loaded, wo_loaded = sem("small_loaded"), sem("raw_loaded"), sem("wo_loaded")
        gu_loaded, d_loaded = sem("gu_loaded"), sem("d_loaded")
        q_out, q_moved, max_moved, out_stored = sem("q_out"), sem("q_moved"), sem("max_moved"), sem("out_stored")
        pool_chain, sim_cleared = sem("pool_chain"), sem("sim_cleared")
        consts_ready, attn_w_ready = sem("consts_ready"), sem("attn_w_ready")
        dve_chain = sem("dve_chain")
        job_filled = sem("job_filled")
        job_copied = sem("job_copied")
        job_drained = [sem("job_drained0"), sem("job_drained1")]
        var_ready, rstd_ready, xn_ready = sem("var_ready"), sem("rstd_ready"), sem("xn_ready")
        router_exp, onehot_ready, cw_ready = sem("router_exp"), sem("onehot_ready"), sem("cw_ready")
        probs_used, pv_read = sem("probs_used"), sem("pv_read")
        gu_done, silu_done, h_ready = sem("gu_done"), sem("silu_done"), sem("h_ready")
        tr_done, ht_hi_ready, ht_ready = sem("tr_done"), sem("ht_hi_ready"), sem("ht_ready")
        dn_done, x_added = sem("dn_done"), sem("x_added")

        block = ctx.enter_context(nc.Block())

        def base(b):
            return 64 * (b % 2)

        def filled(eng, step, i=0):
            eng.wait_ge(job_filled, JOB[step, i] + 1)

        def drained(eng, step, i=0):
            j = JOB[step, i]
            eng.wait_ge(job_drained[j % 2], j // 2 + 1)

        def job_bank(step, i=0):
            return job_banks[JOB[step, i] % 2][:, :]

        def drained_sem(step, i=0):
            return job_drained[JOB[step, i] % 2]

        def prep_parts(s, bank_):
            if s < RB // 2:
                return [(raw_gu[:, 2 * s + r, k * P:(k + 1) * P], bank_[:, (k * 2 + r) * P:(k * 2 + r + 1) * P])
                        for k in range(KC) for r in range(2)]
            j = s - RB // 2
            flat = raw_d[:, :, :, :].rearrange("p k e f -> p k (e f)")
            return [(flat[:, k, j * P:(j + 1) * P], bank_[:, k * P:(k + 1) * P]) for k in range(KC)]

        def prep_out(w_gu, w_d, s, bank_):
            g, s = s // STEPS, s % STEPS
            if s < RB // 2:
                return (w_gu[:, g, :, 2 * s * P:2 * (s + 1) * P],
                        bank_[:, 0:4 * P].rearrange("p (k n) -> p k n", k=KC))
            return w_d[:, g, s - RB // 2, :], bank_[:, 0:KC * P]

        def sm_chunks(n, c):
            out_ = []
            for i in range(3):
                m = 3 * c + i
                out_.append((i,) + ((0, 4 * m, 4, P) if m < H // 4 else (1, 2 * (m - H // 4), 2, T)))
            return out_

        def walk(slot, step, plain_group, last):
            for name, n in BEFORE:
                step(name, n)
            for u in range(LAST_STEP // BT * BT + BT):
                slot(u, *phase_of(u), False)
                for name, n in AFTER.get(u, ()):
                    step(name, n)
            u = LAST_STEP // BT * BT + BT
            while u < ALL:
                b, g, _ = phase_of(u)
                if g == 0:
                    for i in range(BT):
                        slot(u + i, *phase_of(u + i), True)
                    u, g = u + BT, 1
                plain_group(u - g * BT, b, g)
                u += (G - g) * BT
            last()

        @block.sync
        def _(sp):
            for b in range(B):
                sp.dma_start(x[:, BT * b:BT * (b + 1), :], x_rows[:, BT * b:BT * (b + 1), :]).then_inc(x_loaded[b], 16)
                if b == 0:
                    sp.dma_start(raw_gu[:], gate_up_rows[0]).then_inc(gu_loaded, 16)
                    for k in range(KC):
                        sp.dma_start(raw_d[:, k], down_rows[0, k]).then_inc(d_loaded, 16)
            for g in range(1, G):
                filled(sp, ("PREP", (g - 1) * STEPS + RB // 2 - 1))
                sp.dma_start(raw_gu[:], gate_up_rows[g]).then_inc(gu_loaded, 16)
                filled(sp, ("PREP", g * STEPS - 1))
                for k in range(KC):
                    sp.dma_start(raw_d[:, k], down_rows[g, k]).then_inc(d_loaded, 16)
            for b in range(B):
                drained(sp, ("QK", b), 0)
                if b == 0:
                    filled(sp, ("PREP", G * STEPS - 1))
                if b >= 2:
                    sp.wait_ge(probs_used, HP * (b - 1))
                for m, part in enumerate((q_hi, q_lo)):
                    sp.dma_start(q_dram[b, m].rearrange("p a t -> p (a t)"), part.bitcast(f32)).then_inc(q_out, 16)
                sp.wait_ge(q_out, 32 * (b + 1))
                for row, m in ((0, 0), (D, 1), (2 * D, 0)):
                    for blk in range(H // HB):
                        sp.dma_start(qs[base(b) + row:base(b) + row + D, blk * HB:(blk + 1) * HB, :].bitcast(f32),
                                     q_dram[b, m, :, blk, :].rearrange("(h d) t -> d h t", d=D)).then_inc(q_moved, 16)
                drained(sp, ("SMT", b))
                row = base(b) + 3 * D
                sp.dma_start(qs[row:row + 1, :, :].bitcast(f32), neg_max_t).then_inc(max_moved, 16)
            for t in range(NT):
                b, i = t // BT, t % BT
                sp.wait_ge(x_added, PHASE * (B + b + 1) - BT + i + 1)
                sp.dma_start(out_rows[:, t, :], x[:, t, :]).then_inc(out_stored, 16)
            sp.wait_ge(out_stored, 16 * NT)

        @block.gpsimd
        def _(pool):
            steps = [0]

            def link(ins):
                steps[0] += 1
                ins.then_inc(pool_chain, 1)
                pool.wait_ge(pool_chain, steps[0])

            def rsqrt(n):
                pool.wait_ge(var_ready, n + 1)
                nc.gpsimd.tensor_tensor(rstd[:], var_eps[:], minus_half[:], ALU.pow).then_inc(rstd_ready, 1)

            nc.gpsimd.memset(sim_bd[:], 0.0).then_inc(sim_cleared, 1)
            link(nc.gpsimd.memset(ident[:], 0.0))
            link(nc.gpsimd.memset(minus_half[:], -0.5))
            link(nc.gpsimd.affine_select(out=ident[:], in_=ident[:], compare_op=ALU.not_equal, fill=1.0,
                                         base=0, pattern=[[-1, P]], channel_multiplier=1))
            link(nc.gpsimd.iota(iota[:], pattern=[[1, E]], base=0, channel_multiplier=0,
                                allow_small_or_imprecise_dtypes=True))
            for r in range(PRIM):
                link(nc.gpsimd.memset(rank[:, r:r + 1], float(PRIM - r)))
            link(nc.gpsimd.memset(ones_row, 1.0))
            link(nc.gpsimd.tensor_copy(ident_b[:], ident[:]))
            pool.wait_ge(small_loaded, 16 * (SEC + 2))
            nc.gpsimd.affine_select(out=sim_bd[:], in_=sim_bd[:], compare_op=ALU.not_equal, fill=1.0,
                                    base=0, pattern=[[-1, P]], channel_multiplier=1).then_inc(consts_ready, 1)
            rsqrt(0)
            link(nc.gpsimd.memset(hide_q[:], 0.0))
            link(nc.gpsimd.affine_select(out=hide_q[:], in_=hide_q[:], compare_op=ALU.is_ge, fill=BIG,
                                         base=0, pattern=[[1, P]], channel_multiplier=-1))
            link(nc.gpsimd.memset(hide_k[:], 0.0))
            link(nc.gpsimd.affine_select(out=hide_k[:], in_=hide_k[:], compare_op=ALU.is_ge, fill=BIG,
                                         base=0, pattern=[[-1, P]], channel_multiplier=1))
            link(nc.gpsimd.memset(v1[:, :, :, D:D + 1], 1.0))
            link(nc.gpsimd.memset(ks[32:64, :].bitcast(f32), 1.0))
            link(nc.gpsimd.memset(ks[96:128, :].bitcast(f32), 1.0))
            pool.wait_ge(raw_loaded, 16 * 3)
            link(nc.gpsimd.memset(wk_hi[:].bitcast(f32), 0.0))
            link(nc.gpsimd.memset(wk_lo[:].bitcast(f32), 0.0))
            raw = probs[:, 0, 0:KC * C].rearrange("p (k n) -> p k n", k=KC)
            raw_kv = probs[:, 1, 0:2 * KC * D].rearrange("p (k n) -> p k n", k=KC)
            link(nc.gpsimd.tensor_copy(wq_hi[:], raw))
            link(nc.gpsimd.tensor_tensor(wq_lo[:], raw, wq_hi[:].bitcast(f32), ALU.subtract))
            link(nc.gpsimd.tensor_copy(wv_hi[:], raw_kv[:, :, D:2 * D]))
            link(nc.gpsimd.tensor_tensor(wv_lo[:], raw_kv[:, :, D:2 * D], wv_hi[:].bitcast(f32), ALU.subtract))
            for n in (0, 1, 2, 4, 5, 6):
                cols = slice(n * D, (n + 1) * D)
                link(nc.gpsimd.tensor_copy(wk_hi[:, :, cols], raw_kv[:, :, 0:D]))
                last = nc.gpsimd.tensor_tensor(wk_lo[:, :, cols], raw_kv[:, :, 0:D],
                                               wk_hi[:, :, cols].bitcast(f32), ALU.subtract)
                if n == 6:
                    last.then_inc(attn_w_ready, 1)
                else:
                    link(last)
            for n in range(1, 3 * B):
                rsqrt(n)

        @block.scalar
        def _(act):
            def copy(out_, in_, scale=1.0):
                return nc.scalar.activation(out_, in_, ACT.Copy, scale=scale)

            act.dma_start(attn[0:E, 0, :], gate_w).then_inc(small_loaded, 16)
            act.dma_start(bo_row, bo.rearrange("(a c) -> a c", a=1)).then_inc(small_loaded, 16)
            act.wait_ge(sim_cleared, 1)
            for n in range(SEC):
                act.dma_start(sim_bd[n * E:(n + 1) * E, n * E:(n + 1) * E], sim).then_inc(small_loaded, 16)
            act.dma_start(probs[:, 0, 0:KC * C].rearrange("p (k n) -> p k n", k=KC),
                          wq.rearrange("(k p) n -> p k n", p=P)).then_inc(raw_loaded, 16)
            raw_kv = probs[:, 1, 0:2 * KC * D].rearrange("p (k n) -> p k n", k=KC)
            act.dma_start(raw_kv[:, :, 0:D], wk.rearrange("(k p) n -> p k n", p=P)).then_inc(raw_loaded, 16)
            act.dma_start(raw_kv[:, :, D:2 * D], wv.rearrange("(k p) n -> p k n", p=P)).then_inc(raw_loaded, 16)
            act.dma_start(wo_sb[:], wo.rearrange("(k p) n -> p k n", p=P)).then_inc(wo_loaded, 16)

            def step(name, n):
                me = (name, n)
                if name == "PREP":
                    filled(act, me)
                    o, i = prep_out(wgu_hi, wd_hi, n, job_bank(me))
                    copy(o, i).then_inc(job_copied, 1)
                elif name == "GW":
                    filled(act, me)
                    copy(gw_hi[:].rearrange("p k e -> p (k e)"), job_bank(me)[:, 0:KC * E]).then_inc(job_copied, 1)
                elif name == "LNc":
                    filled(act, me)
                    cols = slice(T * (n % B), T * (n % B + 1))
                    copy(xt_hi[:, :, cols], job_bank(me).rearrange("p (k n) -> p k n", k=KC)).then_inc(job_copied, 1)
                elif name == "R1a":
                    drained(act, me)
                    nc.scalar.activation(pr[:], pr[:], ACT.Exp).then_inc(router_exp, 1)
                elif name == "R2a":
                    filled(act, me)
                    if n >= 1:
                        filled(act, ("R2b", n - 1))
                    copy(onehot_t[:], job_bank(me)[:, 0:P].bitcast(bf16).rearrange("p (i n) -> p i n", i=BT))\
                        .then_inc(drained_sem(me), 1)
                elif name == "QK":
                    filled(act, me, 0)
                    if n >= 1:
                        act.wait_ge(q_out, 32 * n)
                    copy(q_hi, job_bank(me, 0), scale=D ** -0.5).then_inc(job_copied, 1)
                elif name == "SMT":
                    filled(act, me)
                    if n >= 1:
                        act.wait_ge(max_moved, 16 * n)
                    copy(neg_max_t, job_bank(me)[0:H, 0:T]).then_inc(drained_sem(me), 1)
                elif name[0:2] == "PV" and name != f"PV{HP}":
                    w = int(name[2:])
                    if n == 0 and w == 0:
                        act.wait_ge(attn_w_ready, 1)
                    for half, (lo, hi) in enumerate(((0, 2 * T), (2 * T, 3 * T))):
                        filled(act, me, half)
                        if half == 0 and HP * n + w >= 2:
                            act.wait_ge(probs_used, HP * n + w - 1)
                        nc.scalar.activation(probs[:, w % 2, lo:hi], job_bank(me, half)[:, 0:hi - lo], ACT.Exp)\
                            .then_inc(drained_sem(me, half), 1)
                elif name == "OU1":
                    filled(act, me)
                    act.wait_ge(q_out, 32 * min(n + 2, B))
                    copy(attn_t, job_bank(me).rearrange("p (i n) -> p i n", i=BT)).then_inc(drained_sem(me), 1)

            def gate(u, i, loop):
                for a in range(2):
                    act.wait_ge(gu_done, u * 2 + a + 1)
                    if a == 0 and not (isinstance(u, int) and u < 2):
                        act.wait_ge(tr_done, u - 1)
                    src = gu_banks[(2 * i + a) if loop else (2 * u + a) % GU_BANKS]
                    gate_cols = src[:, 0:HC].rearrange("p (e n) -> p e n", e=2)[:, :, 0:F]
                    nc.scalar.activation(h[:, i, 2 * a:2 * a + 2, :], gate_cols, ACT.Silu).then_inc(silu_done, 1)

            def keep_hi(u, i):
                act.wait_ge(tr_done, u + 1)
                if not (isinstance(u, int) and u < 2):
                    act.wait_ge(dn_done, u - 1)
                copy(ht_hi[:, i, :], tr_bank[:, 0:FC * P]).then_inc(ht_hi_ready, 1)

            def slot(u, b, g, i, loop):
                gate(u, i, loop)
                if not (isinstance(u, int) and u < 1):
                    keep_hi(u - 1, 1 - i)

            def plain_group(u0, b, g0):
                with act.Fori(g0, G) as g:
                    for i in range(BT):
                        slot(g * BT + (u0 + i), b, g, i, True)

            walk(slot, step, plain_group, lambda: keep_hi(ALL - 1, 1))

        @block.vector
        def _(dve):
            steps = [0]
            V = nc.vector

            def link(ins):
                steps[0] += 1
                ins.then_inc(dve_chain, 1)
                dve.wait_ge(dve_chain, steps[0])

            four = [P, BT, SEC, PRIM]

            def choose(n, b, oh, w8):
                link(V.tensor_reduce(best[:], cand[:], AX, ALU.max))
                link(V.tensor_tensor(pick[:], cand[:], best[:, :, :, None].to_broadcast(four), ALU.is_equal))
                link(V.tensor_tensor(pick[:], pick[:], rank[:, None, None, :].to_broadcast(four), ALU.mult))
                V.tensor_scalar(best[:], best[:], 0.5, None, ALU.is_ge)
                link(V.tensor_reduce(gain[:], pick[:], AX, ALU.max))
                V.tensor_tensor(moved[:], best[:], w8[:, :, PRIM:TOP], ALU.mult)
                link(V.tensor_tensor(pick[:], pick[:], gain[:, :, :, None].to_broadcast(four), ALU.is_equal))
                V.tensor_tensor(slot_w[:, :, PRIM:TOP], w8[:, :, PRIM:TOP], moved[:], ALU.subtract)
                link(V.tensor_tensor(pick[:], pick[:], moved[:, :, :, None].to_broadcast(four), ALU.mult))
                link(V.tensor_reduce(gain[:], pick[:].rearrange("p i j k -> p i k j"), AX, ALU.add))
                link(V.tensor_tensor(slot_w[:, :, 0:PRIM], w8[:, :, 0:PRIM], gain[:], ALU.add))

            def compare(n, i, oh):
                prod4 = prod.rearrange("p (j k e) -> p j k e", j=SEC, k=PRIM)
                rows = job_bank(("R2b", n))[:, i * P:(i + 1) * P].rearrange("p (j e) -> p j e", j=SEC)
                ins = V.tensor_tensor(prod4, rows[:, :, None, :].to_broadcast([P, SEC, PRIM, E]),
                                      oh[:, i, None, 0:PRIM, :].to_broadcast([P, SEC, PRIM, E]), ALU.mult)
                if i == BT - 1:
                    ins.then_inc(drained_sem(("R2b", n)), 1)
                    drained(dve, ("R2b", n))
                else:
                    link(ins)
                link(V.tensor_reduce(cand[:, i], prod4, AX, ALU.add))

            def step(name, n):
                me = (name, n)
                b, oh, w8 = n % B, onehot[:], top[:]
                if name == "PREP":
                    dve.wait_ge(job_copied, COPY[me] + 1)
                    o, i = prep_out(wgu_lo, wd_lo, n, job_bank(me))
                    o_hi, _ = prep_out(wgu_hi, wd_hi, n, job_bank(me))
                    V.tensor_tensor(o, i, o_hi.bitcast(f32), ALU.subtract).then_inc(drained_sem(me), 1)
                elif name == "GW":
                    dve.wait_ge(job_copied, COPY[me] + 1)
                    V.tensor_tensor(gw_lo[:].rearrange("p k e -> p (k e)"), job_bank(me)[:, 0:KC * E],
                                    gw_hi[:].rearrange("p k e -> p (k e)").bitcast(f32), ALU.subtract)\
                        .then_inc(drained_sem(me), 1)
                elif name == "LNa":
                    if n < B:
                        dve.wait_ge(x_loaded[b], 16)
                    elif n < 2 * B:
                        dve.wait_ge(x_added, PHASE * (b + 1))
                    else:
                        drained(dve, ("OU2", b))
                    for i in range(BT):
                        ins = V.bn_stats(stats[:, i, :], x[:, BT * b + i, :])
                    link(ins)
                    for i in range(BT):
                        ins = V.bn_aggr(mv[:, i, :], stats[:, i, :])
                    link(ins)
                    V.tensor_scalar(var_eps[:], mv[:, :, 1], EPS, None, ALU.add).then_inc(var_ready, 1)
                elif name == "LNb":
                    dve.wait_ge(rstd_ready, SEQ[me] + 1)
                    if n == B - 1:
                        dve.wait_ge(q_out, 32)
                    for i in range(BT):
                        ins = V.tensor_scalar(xn[:, i, :], x[:, BT * b + i, :], mv[:, i, 0:1], rstd[:, i:i + 1],
                                              ALU.subtract, ALU.mult)
                    ins.then_inc(xn_ready, 1)
                elif name == "LNc":
                    dve.wait_ge(job_copied, COPY[me] + 1)
                    cols = slice(T * b, T * (b + 1))
                    V.tensor_tensor(xt_lo[:, :, cols], job_bank(me).rearrange("p (k n) -> p k n", k=KC),
                                    xt_hi[:, :, cols].bitcast(f32), ALU.subtract).then_inc(drained_sem(me), 1)
                    drained(dve, me)
                elif name == "R1a":
                    filled(dve, me)
                    logits = job_bank(me)[:, 0:BT * E].rearrange("p (i e) -> p i e", i=BT)
                    link(V.tensor_reduce(pmax[:], logits, AX, ALU.max))
                    V.tensor_tensor(pr[:], logits, pmax[:, :, None].to_broadcast([P, BT, E]), ALU.subtract)\
                        .then_inc(drained_sem(me), 1)
                elif name == "R1b":
                    dve.wait_ge(router_exp, n + 1)
                    link(V.tensor_reduce(total[:], pr[:], AX, ALU.add))
                    link(V.reciprocal(total[:], total[:]))
                    link(V.tensor_tensor(pr[:], pr[:], total[:, :, None].to_broadcast([P, BT, E]), ALU.mult))
                    for i in range(BT):
                        ins = V.max(w8[:, i, :], pr[:, i, :])
                    link(ins)
                    for i in range(BT):
                        ins = V.max_index(top_i[:, i, :], w8[:, i, :], pr[:, i, :])
                    link(ins)
                    link(V.tensor_copy(top_f[:], top_i[:]))
                elif name == "R1c":
                    if n == 0:
                        dve.wait_ge(consts_ready, 1)
                    V.tensor_tensor(oh, top_f[:, :, :, None].to_broadcast([P, BT, TOP, E]),
                                    iota[:, None, None, :].to_broadcast([P, BT, TOP, E]), ALU.is_equal)\
                        .then_inc(onehot_ready, 1)
                    link(V.tensor_reduce(total[:], w8, AX, ALU.add))
                    link(V.tensor_scalar(total[:], total[:], 1e-12, None, ALU.max))
                    link(V.reciprocal(total[:], total[:]))
                    link(V.tensor_tensor(w8, w8, total[:, :, None].to_broadcast([P, BT, TOP]), ALU.mult))
                elif name == "R2b":
                    filled(dve, me)
                    for i in range(BT):
                        compare(n, i, oh)
                elif name == "R2c":
                    choose(n, b, oh, w8)
                elif name == "R2d":
                    prod8 = prod.rearrange("p (i k e) -> p i k e", i=BT, k=TOP)
                    link(V.tensor_tensor(prod8, oh, slot_w[:, :, :, None].to_broadcast([P, BT, TOP, E]), ALU.mult))
                    V.tensor_reduce(cw[:, BT * b:BT * (b + 1), :], prod8.rearrange("p i k e -> p i e k"), AX, ALU.add)\
                        .then_inc(cw_ready, 1)
                    dve.wait_ge(cw_ready, n + 1)
                elif name == "QK":
                    dve.wait_ge(job_copied, COPY[me] + 1)
                    V.scalar_tensor_tensor(q_lo, job_bank(me, 0), D ** -0.5, q_hi.bitcast(f32),
                                           ALU.mult, ALU.subtract).then_inc(drained_sem(me, 0), 1)
                    filled(dve, me, 1)
                    if n == 0:
                        dve.wait_ge(attn_w_ready, 1)
                    if n >= 2:
                        dve.wait_ge(probs_used, HP * (n - 1))
                    kv = job_bank(me, 1)
                    o = base(n)
                    link(V.tensor_copy(ks[o:o + 3 * D, :], kv[o:o + 3 * D, 0:T]))
                    low = slice(o + 2 * D, o + 3 * D)
                    V.tensor_tensor(ks[low, :], kv[low, 0:T], ks[low, :].bitcast(f32), ALU.subtract)
                    V.tensor_copy(v1[:, n % 2, :, 0:D], kv[:, T:T + BT * D].rearrange("p (i d) -> p i d", i=BT))\
                        .then_inc(drained_sem(me, 1), 1)
                elif name[0:2] == "SM" and name != "SMT":
                    for j, i, hh, heads, width in sm_chunks(n, int(name[2])):
                        filled(dve, me, j)
                        V.tensor_reduce(neg_max[:, i, hh:hh + heads], job_bank(me, j).rearrange("p (a n) -> p a n", a=heads),
                                        AX, ALU.max, negate=True).then_inc(drained_sem(me, j), 1)
                elif name[0:3] == "OUn":
                    half = int(name[3])
                    dve.wait_ge(probs_used, HP * n + (half + 1) * HP // 2)
                    if n >= 1:
                        filled(dve, ("OU1", n - 1))
                    link(V.reciprocal(rsum[:], pv[:, :, :, D]))
                    V.tensor_tensor(attn[:, :, half * P:(half + 1) * P].rearrange("p i (h d) -> p i h d", h=HB),
                                    pv[:, :, :, 0:D], rsum[:, :, :, None].to_broadcast([P, BT, HB, D]), ALU.mult)\
                        .then_inc(pv_read, 1)
                elif name == "OU2":
                    filled(dve, me)
                    tiles = slice(BT * n, BT * (n + 1))
                    V.tensor_tensor(x[:, tiles, :], job_bank(me).rearrange("p (i c) -> p i c", i=BT), x[:, tiles, :],
                                    ALU.add).then_inc(drained_sem(me), 1)

            def weigh(u, b, g, i, loop):
                if isinstance(u, int) and u % PHASE == 0:
                    dve.wait_ge(cw_ready, u // PHASE + 1)
                for a in range(2):
                    dve.wait_ge(silu_done, u * 2 + a + 1)
                    src = gu_banks[(2 * i + a) if loop else (2 * u + a) % GU_BANKS]
                    for e in range(2 * a, 2 * a + 2):
                        up = src[:, (e % 2) * 2 * F + F:(e % 2 + 1) * 2 * F]
                        ins = V.scalar_tensor_tensor(h[:, i, e, :], h[:, i, e, :], cw[:, BT * b + i, bass.ds(g * EG + e, 1)],
                                                     up, ALU.mult, ALU.mult)
                    ins.then_inc(h_ready, 1)

            def keep_lo(u, i):
                dve.wait_ge(ht_hi_ready, u + 1)
                if not (isinstance(u, int) and u < 2):
                    dve.wait_ge(dn_done, u - 1)
                V.tensor_tensor(ht_lo[:, i, :], tr_bank[:, 0:FC * P], ht_hi[:, i, :].bitcast(f32),
                                ALU.subtract).then_inc(ht_ready, 1)

            def add(u, t):
                dve.wait_ge(dn_done, u + 1)
                if not (isinstance(u, int) and u < 2):
                    dve.wait_ge(x_added, u - 1)
                V.scalar_tensor_tensor(x[:, t, :], dn_bank[:, 0:C], 0.5, x[:, t, :], ALU.mult, ALU.add).then_inc(x_added, 1)

            def slot(u, b, g, i, loop):
                weigh(u, b, g, i, loop)
                if not (isinstance(u, int) and u < 1):
                    keep_lo(u - 1, 1 - i)
                if not (isinstance(u, int) and u < 2):
                    b2 = phase_of(u - 2)[0] if isinstance(u, int) else b
                    add(u - 2, BT * b2 + i)

            def plain_group(u0, b, g0):
                with dve.Fori(g0, G) as g:
                    for i in range(BT):
                        slot(g * BT + (u0 + i), b, g, i, True)

            def last():
                keep_lo(ALL - 1, 1)
                add(ALL - 2, NT - 2)
                add(ALL - 1, NT - 1)

            walk(slot, step, plain_group, last)

        @block.tensor
        def _(pe):
            def mm(out_, lhs, rhs, start, stop, **kw):
                return nc.tensor.matmul(out_, lhs, rhs, start=start, stop=stop, **kw)

            def claim(step, i=0):
                j = JOB[step, i]
                if j >= 2:
                    pe.wait_ge(job_drained[j % 2], j // 2)
                return job_banks[j % 2][:, :]

            def split_product(out_, parts):
                for m, (lhs, rhs) in enumerate(parts):
                    ins = mm(out_, lhs, rhs, m == 0, m == len(parts) - 1)
                return ins

            def three(a_hi, a_lo, b_hi, b_lo):
                return [(a_lo, b_hi), (a_hi, b_lo), (a_hi, b_hi)]

            def step(name, n):
                me = (name, n)
                b = n % B
                cols = slice(T * b, T * (b + 1))
                tok = [slice(T * b + i * P, T * b + (i + 1) * P) for i in range(BT)]
                if name == "PREP":
                    if n % STEPS == 0:
                        pe.wait_ge(gu_loaded, 16 * (n // STEPS + 1))
                    if n % STEPS == RB // 2:
                        pe.wait_ge(d_loaded, 16 * KC * (n // STEPS + 1))
                    dst = claim(me)
                    for raw, place in prep_parts(n % STEPS, dst):
                        ins = nc.tensor.transpose(place, raw, ident[:])
                    ins.then_inc(job_filled, 1)
                elif name == "GW":
                    pe.wait_ge(consts_ready, 1)
                    dst = claim(me)
                    for k in range(KC):
                        ins = nc.tensor.transpose(dst[:, k * E:(k + 1) * E], attn[0:E, 0, k * P:(k + 1) * P], ident[0:E, 0:E])
                    ins.then_inc(job_filled, 1)
                elif name == "LNc":
                    dst = claim(me)
                    pe.wait_ge(xn_ready, SEQ[me] + 1)
                    for k in range(KC):
                        for i in range(BT):
                            ins = nc.tensor.transpose(dst[:, (k * BT + i) * P:(k * BT + i + 1) * P],
                                                      xn[:, i, k * P:(k + 1) * P], ident[:])
                    ins.then_inc(job_filled, 1)
                elif name == "R1a":
                    dst = claim(me)
                    drained(pe, ("LNc", n if n < B else n + B))
                    for i in range(BT):
                        ins = split_product(dst[:, i * E:(i + 1) * E],
                                            [(a[:, k, tok[i]], w[:, k, :]) for k in range(KC) for a, w in
                                             ((xt_lo, gw_lo), (xt_lo, gw_hi), (xt_hi, gw_lo), (xt_hi, gw_hi))])
                    ins.then_inc(job_filled, 1)
                elif name == "R2a":
                    flipped = claim(me)[:, 0:P].bitcast(bf16)
                    pe.wait_ge(onehot_ready, n + 1)
                    for i in range(BT):
                        ins = nc.tensor.transpose(flipped[:, i * P:(i + 1) * P],
                                                  onehot[:, i, PRIM:TOP, :].rearrange("p k e -> p (k e)"), ident_b[:])
                    ins.then_inc(job_filled, 1)
                elif name == "R2b":
                    dst = claim(me)
                    drained(pe, ("R2a", n))
                    for i in range(BT):
                        ins = mm(dst[:, i * P:(i + 1) * P], onehot_t[:, i, :], sim_bd[:], True, True)
                    ins.then_inc(job_filled, 1)
                elif name == "QK":
                    dst = claim(me, 0)
                    drained(pe, ("LNc", B + n))
                    if n == 0:
                        pe.wait_ge(attn_w_ready, 1)
                    for blk in range(H // HB):
                        w = slice(blk * P, (blk + 1) * P)
                        ins = split_product(dst[:, blk * T:(blk + 1) * T],
                                            [p_ for k in range(KC) for p_ in
                                             three(wq_hi[:, k, w], wq_lo[:, k, w], xt_hi[:, k, cols], xt_lo[:, k, cols])])
                    ins.then_inc(job_filled, 1)
                    dst = claim(me, 1)
                    split_product(dst[0:7 * D, 0:T], [p_ for k in range(KC) for p_ in
                                                      three(wk_hi[:, k, :], wk_lo[:, k, :], xt_hi[:, k, cols], xt_lo[:, k, cols])])
                    for i in range(BT):
                        ins = split_product(dst[:, T + i * D:T + (i + 1) * D],
                                            [p_ for k in range(KC) for p_ in
                                             three(xt_hi[:, k, tok[i]], xt_lo[:, k, tok[i]], wv_hi[:, k, :], wv_lo[:, k, :])])
                    ins.then_inc(job_filled, 1)
                elif name == "SMT":
                    dst = claim(me)
                    for j in range(3):
                        drained(pe, ("SM3", n), j)
                    for i in range(BT):
                        ins = nc.tensor.transpose(dst[0:H, i * P:(i + 1) * P], neg_max[:, i, :], ident[:])
                    ins.then_inc(job_filled, 1)
                elif name[0:2] == "SM":
                    if name == "SM0":
                        pe.wait_ge(q_moved, 16 * MOVES * (n + 1))
                        drained(pe, ("QK", n), 1)
                    rows = slice(base(n), base(n) + 3 * D)
                    for j, i, hh, heads, width in sm_chunks(n, int(name[2])):
                        dst = claim(me, j)
                        mm(dst.rearrange("p (a n) -> p a n", a=heads)[:, :, width - P:width], hide_q[:],
                           ident_b[:, None, :].to_broadcast([P, heads, P]), True, False, skip_group_check=True)
                        for a in range(heads):
                            ins = mm(dst[:, a * width:(a + 1) * width], qs[rows, hh + a, i * P:(i + 1) * P],
                                     ks[rows, 0:width], False, a == heads - 1, skip_group_check=True)
                        ins.then_inc(job_filled, 1)
                elif name[0:2] == "PV":
                    w = int(name[2:])
                    if w < HP:
                        scores(n, w)
                    if w >= 1:
                        times_v(n, w - 1)
                elif name == "OU1":
                    dst = claim(me)
                    pe.wait_ge(pv_read, 2 * n + 2)
                    for i in range(BT):
                        for k in range(KC):
                            ins = nc.tensor.transpose(dst[:, (i * KC + k) * P:(i * KC + k + 1) * P],
                                                      attn[:, i, k * P:(k + 1) * P], ident[:])
                    ins.then_inc(job_filled, 1)
                elif name == "OU2":
                    dst = claim(me)
                    if n == 0:
                        pe.wait_ge(wo_loaded, 16)
                    drained(pe, ("OU1", n))
                    for i in range(BT):
                        cols = slice(i * C, (i + 1) * C)
                        mm(dst[:, cols], ones_row, bo_row, True, False)
                        for k in range(KC):
                            ins = mm(dst[:, cols], attn_t[:, i, k * P:(k + 1) * P], wo_sb[:, k, :], False, k == KC - 1)
                    ins.then_inc(job_filled, 1)

            def scores(n, w):
                me = (f"PV{w}", n)
                if w == 0:
                    pe.wait_ge(max_moved, 16 * (n + 1))
                rows = slice(base(n), base(n) + 3 * D + 1)
                heads = slice(2 * w, 2 * w + 2)
                diagonal = ident_b[:, None, :].to_broadcast([P, 2, P])
                dst = claim(me, 0).rearrange("p (a n) -> p a n", a=2)
                mm(dst[:, :, 0:P], hide_k[:], diagonal, True, False, skip_group_check=True)
                mm(dst, ks[rows, 0:P], qs[rows, heads, :], False, True, skip_group_check=True).then_inc(job_filled, 1)
                dst = claim(me, 1)[:, 0:2 * P].rearrange("p (a n) -> p a n", a=2)
                mm(dst, hide_k[:], diagonal, True, False, skip_group_check=True)
                mm(dst, ks[rows, P:T], qs[rows, heads, P:T], False, True, skip_group_check=True).then_inc(job_filled, 1)

            def times_v(n, w):
                me = (f"PV{w}", n)
                for half in range(2):
                    drained(pe, me, half)
                if w % (HP // 2) == 0 and 2 * n + w // (HP // 2) > 0:
                    pe.wait_ge(pv_read, 2 * n + w // (HP // 2))
                v = [v1[:, n % 2, i, :] for i in range(BT)]
                for a in range(2):
                    hh = (2 * w + a) % HB
                    mm(pv[:, 0, hh, :], probs[:, w % 2, a * T:a * T + P], v[0], True, True)
                    mm(pv[:, 1, hh, :], probs[:, w % 2, a * T + P:(a + 1) * T], v[0], True, False)
                    ins = mm(pv[:, 1, hh, :], probs[:, w % 2, 2 * T + a * P:2 * T + (a + 1) * P], v[1], False, True)
                ins.then_inc(probs_used, 1)

            def gate_up_products(u, b, g, i, loop):
                if isinstance(u, int) and u % PHASE == 0:
                    drained(pe, ("LNc", (u // PHASE) if u < B * PHASE else B + u // PHASE))
                if isinstance(u, int) and u < PHASE and i == 0:
                    for s in range(STEPS * (g + 1) - 2, STEPS * (g + 1)):
                        drained(pe, ("PREP", s))
                t = BT * b + i
                tok = slice(t * P, (t + 1) * P)
                for a in range(2):
                    if loop:
                        pe.wait_ge(h_ready, u * 2 + (a - GU_BANKS))
                        dst = gu_banks[2 * i + a]
                    else:
                        if 2 * u + a >= GU_BANKS:
                            pe.wait_ge(h_ready, 2 * u + a - GU_BANKS + 1)
                        dst = gu_banks[(2 * u + a) % GU_BANKS]
                    ac = slice(a * HC, (a + 1) * HC)
                    ins = split_product(dst[:, 0:HC], [p_ for k in range(KC) for p_ in
                                                       three(xt_hi[:, k, tok], xt_lo[:, k, tok], wgu_hi[:, g, k, ac], wgu_lo[:, g, k, ac])])
                    ins.then_inc(gu_done, 1)

            def transpose_h(u, i):
                pe.wait_ge(h_ready, u * 2 + 2)
                if not (isinstance(u, int) and u < 1):
                    pe.wait_ge(ht_ready, u)
                flat = h[:, i].rearrange("p e f -> p (e f)")
                for j in range(FC):
                    ins = nc.tensor.transpose(tr_bank[:, j * P:(j + 1) * P], flat[:, j * P:(j + 1) * P], ident[:])
                ins.then_inc(tr_done, 1)

            def down_products(u, g, i):
                pe.wait_ge(ht_ready, u + 1)
                if not (isinstance(u, int) and u < 1):
                    pe.wait_ge(x_added, u)
                ins = split_product(dn_bank[:, 0:C], [p_ for j in range(FC) for p_ in
                                                      three(ht_hi[:, i, j * P:(j + 1) * P], ht_lo[:, i, j * P:(j + 1) * P],
                                                            wd_hi[:, g, j, :], wd_lo[:, g, j, :])])
                ins.then_inc(dn_done, 1)

            def slot(u, b, g, i, loop):
                gate_up_products(u, b, g, i, loop)
                if not (isinstance(u, int) and u < 1):
                    transpose_h(u - 1, 1 - i)
                if not (isinstance(u, int) and u < 2):
                    down_products(u - 2, phase_of(u - 2)[1] if isinstance(u, int) else g - 1, i)

            def plain_group(u0, b, g0):
                start = u0 + g0 * BT
                pe.wait_ge(h_ready, 2 * start)
                with pe.Fori(g0, G) as g:
                    for i in range(BT):
                        slot(g * BT + (u0 + i), b, g, i, True)

            def last():
                transpose_h(ALL - 1, 1)
                down_products(ALL - 2, G - 1, 0)
                down_products(ALL - 1, G - 1, 1)

            walk(slot, step, plain_group, last)


_INS = ["L0_attn_x", "L0_attn_Wq", "L0_attn_Wk", "L0_attn_Wv", "L0_attn_Wo", "L0_attn_bo",
        "L0_ffn_gate_weight", "L0_ffn_gate_up_proj", "L0_ffn_down_proj", "L0_ffn_similarity"]


def kernel(**inputs):
    import numpy as _np
    import concourse.bacc as _bacc
    from concourse import mybir as _mybir
    from concourse.bass_utils import run_bass_kernel_spmd as _run

    nc = _bacc.Bacc("TRN2", target_bir_lowering=False, num_devices=1, dynamic_dma_scratch_size=256)
    arrays, args = {}, []
    for name in _INS:
        a = _np.ascontiguousarray(inputs[name])
        arrays[f"in_{name}"] = a
        args.append(nc.dram_tensor(f"in_{name}", a.shape, _mybir.dt.from_np(a.dtype), kind="ExternalInput").ap())
    args.append(nc.dram_tensor("out_x", (B, T, C), _mybir.dt.float32, kind="ExternalOutput").ap())
    macaron(nc, *args)
    r = _run(nc, [arrays], core_ids=[0])
    return r.results[0]["out_x"]
```

```python
import concourse.bass as bass
from concourse import mybir
from contextlib import ExitStack

P = 128
B, T, C = 4, 256, 256
NT = B * T // P
BT = T // P
KC = C // P
E, F = 32, 96
TOP, PRIM = 8, 4
SEC = TOP - PRIM
H, D = 16, 16
HB = P // D
EG = 4
G = E // EG
GC = EG * 2 * F
HC = GC // 2
FC = EG * F // P
RB = GC // P
STEPS = RB // 2 + FC
BIG = -1.0e30
EPS = 1e-5
HP = H // 2
HG = 4
VC = 3 * D + 1
SHIFT = 8.0
SMS = H // 4 + H // 2
MOVES = 3 * (H // HB)
PHASE = G * BT
ALL = 2 * B * PHASE
GU_BANKS = 3

JOBS_OF = {"GW": 1, "LNc": 1, "R1a": 1, "R1t": 1, "R2a": 1, "R2b0": 1, "R2b1": 1, "QK": 2, "VT": 1, "SMT": 1,
           "OU1": 1, "OU2": 1, "PREP": 1} | {f"PS{w}": 2 for w in range(HP)} | {f"SM{m}": 1 for m in range(SMS)}
SPLIT = ("GW", "LNc", "QK", "PREP", "SMT")

PARTS = 4
LN = (("LNa", 0), ("LNb", 2), ("LNc", 5))
ROUTE = (("R1a", 9), ("R1t", 13), ("R1b", 16), ("R1c", 19), ("R2a", 21),
         ("R2b0", 24), ("R2b1", 25), ("R2c", 27), ("R2d", 32))
SM_AT, SM_EVERY, PS_AT = 21, 1, 47
ATTEND = ((("QK", 8), ("VT", 10))
          + tuple((f"SM{m}", SM_AT + SM_EVERY * m) for m in range(SMS)) + (("SMT", SM_AT + SM_EVERY * SMS),)
          + tuple((f"PV{w}", PS_AT + PARTS * (w + 1)) for w in range(HP))
          + tuple((f"PS{w}", PS_AT + PARTS * w) for w in range(HP))
          + tuple((f"OUn{i}", PS_AT + PARTS * 2 * (i + 1)) for i in range(H // HG))
          + (("OU1", PS_AT + PARTS * HP + 2), ("OU2", PS_AT + PARTS * HP + 5)))
AGAIN = PS_AT + PARTS * HP + 8
FIRST_ROUTER = {1: 1, 2: 36, 3: 90}
PREPS_BEFORE = 3
FIRST_PREPS = (0, 0, 1, 2, 3, 3, 5, 6, 7)
PREP_PARTS = (0, 2, 3)


def make_schedule():
    before = [("LNa", 0), ("GW", 0), ("LNb", 0), ("LNc", 0), ("R1a", 0), ("R1t", 0),
              ("R1b", 0), ("PREP", 0), ("R1c", 0), ("PREP", 1), ("R2a", 0), ("R2b0", 0),
              ("R2b1", 0), ("PREP", 2), ("R2c", 0), ("R2d", 0)]
    after = {}
    for b, start in FIRST_ROUTER.items():
        for name, off in LN + ROUTE:
            after.setdefault(start + off, []).append((name, b))
    for b in range(B):
        start = PARTS * (PHASE * (b + 1) + 2) - 1
        for name, off in LN:
            after.setdefault(start + off, []).append((name, B + b))
            after.setdefault(start + AGAIN + off, []).append((name, 2 * B + b))
        for name, off in ATTEND:
            after.setdefault(start + off, []).append((name, b))
        for name, off in ROUTE:
            after.setdefault(start + AGAIN + off, []).append((name, B + b))
    for s, part in zip(range(PREPS_BEFORE, 2 * STEPS), FIRST_PREPS):
        after.setdefault(part, []).append(("PREP", s))
    per_slot = len(PREP_PARTS)
    for m in range(STEPS, STEPS * (G - 1)):
        after.setdefault(PARTS * (m // per_slot) + PREP_PARTS[m % per_slot], []).append(("PREP", STEPS + m))
    return before, after


BEFORE, AFTER = make_schedule()
TANH_SLOTS = {part // PARTS for part in AFTER for name, _ in AFTER[part] if name[0:2] == "PS"}
PLAIN = (max(AFTER) // PARTS // BT + 1) * BT
ORDER = BEFORE + [step for part in sorted(AFTER) for step in AFTER[part]]


def buffer_users(names):
    users = [step for step in ORDER if step[0] in names]
    return dict(zip(users[1:], users))


WORK_BEFORE = buffer_users(("LNb", "LNc", "QK", "R2b0", "R2b1", "R2d", "OU1", "OU2"))
for partner, name in (("LNb", "LNc"), ("OU1", "OU2")):
    assert all(before[0] == partner for step, before in WORK_BEFORE.items() if step[0] == name)
for chain in (("LNa", "LNb", "LNc"), ("R1a", "R1t", "R1b", "R1c", "R2a", "R2b0", "R2b1", "R2c", "R2d")):
    assert all(before[0] == chain[chain.index(step[0]) - 1] for step, before in buffer_users(chain).items())


def number_jobs():
    job, copy, seq, pv_jobs, jobs, copies, seen = {}, {}, {}, {}, 0, 0, {}
    on_bank, bank, held, batches = [0, 0, 0], 0, False, 0
    for step in ORDER:
        for i in range(JOBS_OF.get(step[0], 0)):
            bank = (bank + 1) % (2 if held else 3)
            job[step, i] = jobs, bank, on_bank[bank], batches
            on_bank[bank] += 1
            jobs += 1
        if step[0] == "PV0":
            held, pv_jobs[step[1]] = True, on_bank[2]
        elif step[0] == f"OUn{H // HG - 1}":
            held, batches = False, batches + 1
        if step[0] in SPLIT:
            copy[step] = copies
            copies += 1
        seq[step] = seen.get(step[0], 0)
        seen[step[0]] = seq[step] + 1
    return job, copy, seq, pv_jobs


JOB, COPY, SEQ, PV_JOBS = number_jobs()


def phase_of(u):
    return u // PHASE % B, u % PHASE // BT, u % BT


def macaron(nc, x_in, wq, wk, wv, wo, bo, gate_w, gate_up, down, sim, out):
    f32, f32r, u32 = mybir.dt.float32, mybir.dt.float32r, mybir.dt.uint32
    bf16, f16 = mybir.dt.bfloat16, mybir.dt.float16
    ALU, ACT, AX = mybir.AluOpType, mybir.ActivationFunctionType, mybir.AxisListType.X

    x_rows = x_in.rearrange("b (i p) c -> p (b i) c", p=P)
    out_rows = out.rearrange("b (i p) c -> p (b i) c", p=P)
    gate_up_rows = gate_up.rearrange("(g e) f c -> g (e f) c", g=G).rearrange("g (r p) c -> g p r c", p=P)
    down_rows = down.rearrange("(g e) (h p) f -> g h p e f", g=G, p=P)
    q_dram = nc.dram_tensor("q_dram", (B, 2, P, H // HB, T), f32, kind="Internal").ap()

    with ExitStack() as ctx:
        def sb(name, shape, dt, stack=ctx):
            return stack.enter_context(nc.sbuf_tensor(name, shape, dt))

        def sem(name):
            return ctx.enter_context(nc.semaphore(name))

        x = sb("x", [P, NT, C], f32)
        xt_hi = sb("xt_hi", [P, KC, B * T], f32r)
        xt_lo = sb("xt_lo", [P, KC, B * T], f32r)
        wgu_hi = sb("wgu_hi", [P, G, KC, GC], f32r)
        wgu_lo = sb("wgu_lo", [P, G, KC, GC], f32r)
        wd_hi = sb("wd_hi", [P, G, FC, C], f32r)
        wd_lo = sb("wd_lo", [P, G, FC, C], f32r)
        h = sb("h", [P, 2, EG, F], f32)
        ht_hi = sb("ht_hi", [P, 2, FC * P], f32r)
        ht_lo = sb("ht_lo", [P, 2, FC * P], f32r)
        cw = sb("cw", [P, NT, E], f32)
        with ExitStack() as first_phase:
            raw_gu = sb("raw_gu", [P, RB, C], f32, first_phase)
            raw_d = sb("raw_d", [P, KC, EG, F], f32, first_phase)
        qs = sb("qs", [P, H, T], f32r)
        probs = sb("probs", [P, 3 * T], f32)
        p_hi, p_lo = sb("p_hi", [P, 3 * T], f16), sb("p_lo", [P, 3 * T], f16)
        work = sb("work", [P, 2, 2 * T], f32)
        xn = work[:, 0, :].rearrange("p (i c) -> p i c", i=BT)
        attn_t, prod = xn, work[:, 0, :]
        q_hi, q_lo = work[:, 0, :].bitcast(f32r), work[:, 1, :].bitcast(f32r)
        wq_hi, wq_lo = sb("wq_hi", [P, KC, C], f32r), sb("wq_lo", [P, KC, C], f32r)
        wkv_hi, wkv_lo = sb("wkv_hi", [P, KC, P], f32r), sb("wkv_lo", [P, KC, P], f32r)
        wo_sb = sb("wo_sb", [P, KC, C], f32)
        rows_ = sb("rows_", [P, C + P], f32)
        neg_hi = rows_[0:H, 0:T].bitcast(f32r)
        v_t = rows_[P - 2 * D:P, 0:T]
        bo_row, ones_row = rows_[32:33, 0:C], rows_[32:33, C:C + P]
        ks = sb("ks", [P, T], f32r)
        v_raw = sb("v_raw", [P, BT, D], f32)
        v3 = sb("v3", [P, 2, BT, VC], bf16)
        neg_max = sb("neg_max", [P, BT, H], f32)
        attn = sb("attn", [P, BT, C], f32)
        neg_lo = attn[0:H, 0, 0:T].bitcast(f32r)
        rsum, summed = sb("rsum", [P, BT, HG], f32), sb("summed", [P, BT, HG, D], f32)
        ident = sb("ident", [P, P], f32)
        ident_b = sb("ident_b", [P, P], bf16)
        hide_q = sb("hide_q", [P, P], bf16)
        hide_k = sb("hide_k", [P, P], bf16)
        iota = sb("iota", [P, E], f32)
        rank = sb("rank", [P, PRIM], f32)
        minus_half = sb("minus_half", [P, BT], f32)
        stats, mv = sb("stats", [P, BT, 6], f32), sb("mv", [P, BT, 2], f32)
        var_eps, rstd = sb("var_eps", [P, BT], f32), sb("rstd", [P, BT], f32)
        gw_hi, gw_lo = sb("gw_hi", [P, KC, E], f32r), sb("gw_lo", [P, KC, E], f32r)
        sim_bd = sb("sim_bd", [P, P], f32)
        pr = sb("pr", [P, BT, E], f32)
        pmax, total = sb("pmax", [P, BT], f32), sb("total", [P, BT], f32)
        top = sb("top", [P, BT, TOP], f32)
        top_i, top_f = sb("top_i", [P, BT, TOP], u32), sb("top_f", [P, BT, TOP], f32)
        onehot = sb("onehot", [P, BT, TOP, E], bf16)
        onehot_t = sb("onehot_t", [P, BT, P], f32)
        logits_t = onehot_t[0:E, :, :].rearrange("p i n -> p (i n)")
        cand = sb("cand", [P, BT, SEC, PRIM], f32)
        pick = sb("pick", [P, BT, SEC, PRIM], f32)
        best, moved = sb("best", [P, BT, SEC], f32), sb("moved", [P, BT, SEC], f32)
        gain, slot_w = sb("gain", [P, BT, PRIM], f32), sb("slot_w", [P, BT, TOP], f32)

        def bank(name):
            return ctx.enter_context(nc.psum_tensor(name, [P, 512], f32))
        gu_banks = [bank(f"gu{i}") for i in range(GU_BANKS)]
        tr_bank, dn_bank, pv_bank = bank("tr"), bank("dn"), bank("pv")
        job_banks = [bank("job0"), bank("job1"), pv_bank]
        gu_banks.append(job_banks[0])
        pv = pv_bank[:, 0:BT * HG * VC].rearrange("p (i h d) -> p i h d", i=BT, h=HG)

        x_loaded = [sem(f"x_loaded{b}") for b in range(B)]
        gate_loaded, sim_loaded = sem("gate_loaded"), sem("sim_loaded")
        raw_loaded, wo_loaded = sem("raw_loaded"), sem("wo_loaded")
        gu_loaded, d_loaded = sem("gu_loaded"), sem("d_loaded")
        q_out, q_moved, max_moved, out_stored = sem("q_out"), sem("q_moved"), sem("max_moved"), sem("out_stored")
        pool_chain, sim_cleared = sem("pool_chain"), sem("sim_cleared")
        ident_ready, consts_ready, attn_w_ready = sem("ident_ready"), sem("consts_ready"), sem("attn_w_ready")
        dve_chain = sem("dve_chain")
        job_filled = sem("job_filled")
        job_copied = sem("job_copied")
        job_drained = [sem(f"job_drained{i}") for i in range(3)]
        var_ready, rstd_ready, xn_ready = sem("var_ready"), sem("rstd_ready"), sem("xn_ready")
        router_exp, onehot_ready, cw_ready = sem("router_exp"), sem("onehot_ready"), sem("cw_ready")
        p_hi_ready, p_ready = sem("p_hi_ready"), sem("p_ready")
        v_t_ready, v_ready = sem("v_t_ready"), sem("v_ready")
        probs_used, pv_read = sem("probs_used"), sem("pv_read")
        gu_done, gate_done = sem("gu_done"), sem("gate_done")
        h_ready = sem("h_ready")
        tr_done, ht_hi_ready, ht_ready = sem("tr_done"), sem("ht_hi_ready"), sem("ht_ready")
        dn_done, x_added = sem("dn_done"), sem("x_added")

        block = ctx.enter_context(nc.Block())

        def base(b):
            return 64 * (b % 2)

        def filled(eng, step, i=0):
            eng.wait_ge(job_filled, JOB[step, i][0] + 1)

        def drained(eng, step, i=0):
            _, bank_, before, _ = JOB[step, i]
            eng.wait_ge(job_drained[bank_], before + 1)

        def job_bank(step, i=0):
            return job_banks[JOB[step, i][1]][:, :]

        def drained_sem(step, i=0):
            return job_drained[JOB[step, i][1]]

        def prep_parts(s, bank_):
            if s < RB // 2:
                return [(raw_gu[:, 2 * s + r, k * P:(k + 1) * P], bank_[:, (k * 2 + r) * P:(k * 2 + r + 1) * P])
                        for k in range(KC) for r in range(2)]
            j = s - RB // 2
            flat = raw_d[:, :, :, :].rearrange("p k e f -> p k (e f)")
            return [(flat[:, k, j * P:(j + 1) * P], bank_[:, k * P:(k + 1) * P]) for k in range(KC)]

        def prep_out(w_gu, w_d, s, bank_):
            g, s = s // STEPS, s % STEPS
            if s < RB // 2:
                return (w_gu[:, g, :, 2 * s * P:2 * (s + 1) * P],
                        bank_[:, 0:4 * P].rearrange("p (k n) -> p k n", k=KC))
            return w_d[:, g, s - RB // 2, :], bank_[:, 0:KC * P]

        def sm_chunk(m):
            return (0, 4 * m, 4, P) if m < H // 4 else (1, 2 * (m - H // 4), 2, T)

        def work_free(eng, me):
            prev = WORK_BEFORE.get(me)
            if prev is None:
                return
            name, n = prev
            if name in ("LNc", "OU2"):
                filled(eng, prev)
            elif name in ("R2b0", "R2b1"):
                drained(eng, prev)
            elif name == "R2d":
                eng.wait_ge(cw_ready, n + 1)
            elif name == "QK":
                eng.wait_ge(q_out, 32 * (n + 1))

        def walk(part, step, plain_group, last):
            def slot(u, loop):
                for q in range(PARTS):
                    part(q, u, *phase_of(u), loop)
                    for name, n in AFTER.get(PARTS * u + q, ()):
                        step(name, n)

            for name, n in BEFORE:
                step(name, n)
            for v in range(PLAIN):
                slot(v, False)
            u = PLAIN
            while u < ALL:
                b, g, _ = phase_of(u)
                if g == 0:
                    for i in range(BT):
                        slot(u + i, True)
                    u, g = u + BT, 1
                plain_group(u - g * BT, b, g)
                u += (G - g) * BT
            last()

        @block.sync
        def _(sp):
            for b in range(B):
                sp.dma_start(x[:, BT * b:BT * (b + 1), :], x_rows[:, BT * b:BT * (b + 1), :]).then_inc(x_loaded[b], 16)
                if b == 0:
                    sp.wait_ge(sim_cleared, 1)
                    for n in range(SEC):
                        sp.dma_start(sim_bd[n * E:(n + 1) * E, n * E:(n + 1) * E], sim).then_inc(sim_loaded, 16)
                    sp.dma_start(raw_gu[:], gate_up_rows[0]).then_inc(gu_loaded, 16)
                    for k in range(KC):
                        sp.dma_start(raw_d[:, k], down_rows[0, k]).then_inc(d_loaded, 16)
            sp.dma_start(bo_row, bo.rearrange("(a c) -> a c", a=1)).then_inc(wo_loaded, 16)
            sp.dma_start(wo_sb[:], wo.rearrange("(k p) n -> p k n", p=P)).then_inc(wo_loaded, 16)
            sp.dma_start(probs[:, 0:KC * C].rearrange("p (k n) -> p k n", k=KC),
                         wq.rearrange("(k p) n -> p k n", p=P)).then_inc(raw_loaded, 16)
            raw_kv = probs[:, KC * C:KC * (C + 2 * D)].rearrange("p (k n) -> p k n", k=KC)
            sp.dma_start(raw_kv[:, :, 0:D], wk.rearrange("(k p) n -> p k n", p=P)).then_inc(raw_loaded, 16)
            sp.dma_start(raw_kv[:, :, D:2 * D], wv.rearrange("(k p) n -> p k n", p=P)).then_inc(raw_loaded, 16)
            for g in range(1, G):
                filled(sp, ("PREP", (g - 1) * STEPS + RB // 2 - 1))
                sp.dma_start(raw_gu[:], gate_up_rows[g]).then_inc(gu_loaded, 16)
                filled(sp, ("PREP", g * STEPS - 1))
                for k in range(KC):
                    sp.dma_start(raw_d[:, k], down_rows[g, k]).then_inc(d_loaded, 16)
            for b in range(B):
                drained(sp, ("QK", b), 0)
                if b == 0:
                    filled(sp, ("PREP", G * STEPS - 1))
                if b >= 2:
                    sp.wait_ge(probs_used, HP * (b - 1))
                for m, part in enumerate((q_hi, q_lo)):
                    sp.dma_start(q_dram[b, m].rearrange("p a t -> p (a t)"), part.bitcast(f32)).then_inc(q_out, 16)
                sp.wait_ge(q_out, 32 * (b + 1))
                for row, m in ((0, 0), (D, 1), (2 * D, 0)):
                    for blk in range(H // HB):
                        sp.dma_start(qs[base(b) + row:base(b) + row + D, blk * HB:(blk + 1) * HB, :].bitcast(f32),
                                     q_dram[b, m, :, blk, :].rearrange("(h d) t -> d h t", d=D)).then_inc(q_moved, 16)
                drained(sp, ("SMT", b))
                for m, part in enumerate((neg_hi, neg_lo)):
                    row = base(b) + 3 * D + m
                    sp.dma_start(qs[row:row + 1, :, :].bitcast(f32), part.bitcast(f32)).then_inc(max_moved, 16)
            for t in range(NT):
                b, i = t // BT, t % BT
                sp.wait_ge(x_added, PHASE * (B + b + 1) - BT + i + 1)
                sp.dma_start(out_rows[:, t, :], x[:, t, :]).then_inc(out_stored, 16)
            sp.wait_ge(out_stored, 16 * NT)

        @block.gpsimd
        def _(pool):
            steps = [0]

            def link(ins):
                steps[0] += 1
                ins.then_inc(pool_chain, 1)
                pool.wait_ge(pool_chain, steps[0])

            def rsqrt(n):
                pool.wait_ge(var_ready, n + 1)
                nc.gpsimd.tensor_tensor(rstd[:], var_eps[:], minus_half[:], ALU.pow).then_inc(rstd_ready, 1)

            nc.gpsimd.memset(sim_bd[:], 0.0).then_inc(sim_cleared, 1)
            link(nc.gpsimd.memset(ident[:], 0.0))
            link(nc.gpsimd.memset(minus_half[:], -0.5))
            link(nc.gpsimd.affine_select(out=ident[:], in_=ident[:], compare_op=ALU.not_equal, fill=1.0,
                                         base=0, pattern=[[-1, P]], channel_multiplier=1))
            nc.gpsimd.tensor_copy(ident_b[:], ident[:]).then_inc(ident_ready, 1)
            link(nc.gpsimd.iota(iota[:], pattern=[[1, E]], base=0, channel_multiplier=0,
                                allow_small_or_imprecise_dtypes=True))
            for r in range(PRIM):
                link(nc.gpsimd.memset(rank[:, r:r + 1], float(PRIM - r)))
            link(nc.gpsimd.memset(ones_row, 1.0))
            rsqrt(0)
            pool.wait_ge(sim_loaded, 16 * SEC)
            nc.gpsimd.affine_select(out=sim_bd[:], in_=sim_bd[:], compare_op=ALU.not_equal, fill=1.0,
                                    base=0, pattern=[[-1, P]], channel_multiplier=1).then_inc(consts_ready, 1)
            link(nc.gpsimd.memset(hide_q[:], 0.0))
            link(nc.gpsimd.affine_select(out=hide_q[:], in_=hide_q[:], compare_op=ALU.is_ge, fill=BIG,
                                         base=0, pattern=[[1, P]], channel_multiplier=-1))
            link(nc.gpsimd.memset(hide_k[:], 0.0))
            link(nc.gpsimd.affine_select(out=hide_k[:], in_=hide_k[:], compare_op=ALU.is_ge, fill=BIG,
                                         base=0, pattern=[[-1, P]], channel_multiplier=1))
            link(nc.gpsimd.memset(v3[:, :, :, 3 * D:VC], 1.0))
            link(nc.gpsimd.memset(ks[32:64, :].bitcast(f32), 1.0))
            link(nc.gpsimd.memset(ks[96:128, :].bitcast(f32), 1.0))
            pool.wait_ge(raw_loaded, 16 * 3)
            link(nc.gpsimd.memset(wkv_hi[:].bitcast(f32), 0.0))
            link(nc.gpsimd.memset(wkv_lo[:].bitcast(f32), 0.0))
            raw = probs[:, 0:KC * C].rearrange("p (k n) -> p k n", k=KC)
            raw_kv = probs[:, KC * C:KC * (C + 2 * D)].rearrange("p (k n) -> p k n", k=KC)
            link(nc.gpsimd.tensor_copy(wq_hi[:], raw))
            link(nc.gpsimd.tensor_tensor(wq_lo[:], raw, wq_hi[:].bitcast(f32), ALU.subtract))
            for n in (0, 1, 2, 4, 5, 6, 7):
                cols = slice(n * D, (n + 1) * D)
                raw = raw_kv[:, :, D:2 * D] if n == 7 else raw_kv[:, :, 0:D]
                link(nc.gpsimd.tensor_copy(wkv_hi[:, :, cols], raw))
                last = nc.gpsimd.tensor_tensor(wkv_lo[:, :, cols], raw, wkv_hi[:, :, cols].bitcast(f32), ALU.subtract)
                if n == 7:
                    last.then_inc(attn_w_ready, 1)
                else:
                    link(last)

            def split_v(n):
                drained(pool, ("VT", n))
                if n >= 2:
                    pool.wait_ge(probs_used, HP * (n - 1))
                a, b, c = (v3[:, n % 2, :, m * D:(m + 1) * D] for m in range(3))
                link(nc.gpsimd.tensor_copy(a, v_raw[:]))
                link(nc.gpsimd.tensor_tensor(v_raw[:], v_raw[:], a, ALU.subtract))
                link(nc.gpsimd.tensor_copy(b, v_raw[:]))
                nc.gpsimd.tensor_tensor(c, v_raw[:], b, ALU.subtract).then_inc(v_ready, 1)

            def rest_of_probs(m):
                pool.wait_ge(p_hi_ready, m + 1)
                if m >= 1:
                    pool.wait_ge(probs_used, m)
                nc.gpsimd.tensor_tensor(p_lo[:], probs[:], p_hi[:], ALU.subtract).then_inc(p_ready, 1)

            for name, n in ORDER[1:]:
                if name == "LNa":
                    rsqrt(SEQ[name, n])
                elif name[0:2] == "PS":
                    rest_of_probs(HP * n + int(name[2:]))
                elif name == "VT":
                    split_v(n)

        @block.scalar
        def _(act):
            def copy(out_, in_, scale=1.0):
                return nc.scalar.activation(out_, in_, ACT.Copy, scale=scale)

            act.dma_start(attn[0:E, 0, :], gate_w).then_inc(gate_loaded, 16)

            def step(name, n):
                me = (name, n)
                if name == "PREP":
                    filled(act, me)
                    o, i = prep_out(wgu_hi, wd_hi, n, job_bank(me))
                    copy(o, i).then_inc(job_copied, 1)
                elif name == "GW":
                    filled(act, me)
                    copy(gw_hi[:].rearrange("p k e -> p (k e)"), job_bank(me)[:, 0:KC * E]).then_inc(job_copied, 1)
                elif name == "LNc":
                    filled(act, me)
                    cols = slice(T * (n % B), T * (n % B + 1))
                    copy(xt_hi[:, :, cols], job_bank(me).rearrange("p (k n) -> p k n", k=KC)).then_inc(job_copied, 1)
                elif name == "R1a":
                    filled(act, me)
                    if n >= 1:
                        filled(act, ("R2b1", n - 1))
                    copy(logits_t, job_bank(me)[0:E, 0:T]).then_inc(drained_sem(me), 1)
                elif name == "R1t":
                    drained(act, me)
                    nc.scalar.activation(pr[:], pr[:], ACT.Exp).then_inc(router_exp, 1)
                elif name == "R2a":
                    filled(act, me)
                    copy(onehot_t[:], job_bank(me)[:, 0:P].bitcast(bf16).rearrange("p (i n) -> p i n", i=BT))\
                        .then_inc(drained_sem(me), 1)
                elif name == "QK":
                    filled(act, me, 0)
                    work_free(act, me)
                    copy(q_hi, job_bank(me, 0), scale=D ** -0.5).then_inc(job_copied, 1)
                    filled(act, me, 1)
                    if n >= 1:
                        filled(act, ("VT", n - 1))
                    copy(v_t, job_bank(me, 1)[P - 2 * D:P, 0:T]).then_inc(v_t_ready, 1)
                elif name == "SMT":
                    filled(act, me)
                    if n >= 1:
                        act.wait_ge(max_moved, 32 * n)
                    nc.scalar.activation(neg_hi, job_bank(me)[0:H, 0:T], ACT.Copy, bias=SHIFT).then_inc(job_copied, 1)
                elif name[0:2] == "PS":
                    w = int(name[2:])
                    if n == 0 and w == 0:
                        act.wait_ge(attn_w_ready, 1)
                    for half, (lo, hi) in enumerate(((0, 2 * T), (2 * T, 3 * T))):
                        filled(act, me, half)
                        if half == 0 and HP * n + w >= 1:
                            act.wait_ge(p_ready, HP * n + w)
                        nc.scalar.activation(probs[:, lo:hi], job_bank(me, half)[:, 0:hi - lo], ACT.Exp)\
                            .then_inc(drained_sem(me, half), 1)
                    for half in range(2):
                        drained(act, me, half)
                    if HP * n + w >= 1:
                        act.wait_ge(probs_used, HP * n + w)
                    copy(p_hi[:], probs[:]).then_inc(p_hi_ready, 1)
                elif name == "OU1":
                    filled(act, me)
                    work_free(act, me)
                    copy(attn_t, job_bank(me).rearrange("p (i n) -> p i n", i=BT)).then_inc(drained_sem(me), 1)

            def gate(a, u, i, loop):
                act.wait_ge(gu_done, u * 2 + a + 1)
                if a == 0 and not (isinstance(u, int) and u < 2):
                    act.wait_ge(tr_done, u - 1)
                src = gu_banks[(2 * i + a) if loop else (2 * u + a) % GU_BANKS]
                gate_cols = src[:, 0:HC].rearrange("p (e n) -> p e n", e=2)[:, :, 0:F]
                if isinstance(u, int) and u in TANH_SLOTS:
                    nc.scalar.activation(h[:, i, 2 * a:2 * a + 2, :], gate_cols, ACT.Tanh, scale=0.5).then_inc(gate_done, 1)
                else:
                    nc.scalar.activation(h[:, i, 2 * a:2 * a + 2, :], gate_cols, ACT.Silu).then_inc(gate_done, 1)

            def keep_hi(u, i):
                act.wait_ge(tr_done, u + 1)
                if not (isinstance(u, int) and u < 2):
                    act.wait_ge(dn_done, u - 1)
                copy(ht_hi[:, i, :], tr_bank[:, 0:FC * P]).then_inc(ht_hi_ready, 1)

            def part(q, u, b, g, i, loop):
                if q < 2:
                    gate(q, u, i, loop)
                elif q == 2 and not (isinstance(u, int) and u < 1):
                    keep_hi(u - 1, 1 - i)

            def plain_group(u0, b, g0):
                with act.Fori(g0, G) as g:
                    for i in range(BT):
                        for q in range(PARTS):
                            part(q, g * BT + (u0 + i), b, g, i, True)

            walk(part, step, plain_group, lambda: keep_hi(ALL - 1, 1))

        @block.vector
        def _(dve):
            steps = [0]
            V = nc.vector

            def link(ins):
                steps[0] += 1
                ins.then_inc(dve_chain, 1)
                dve.wait_ge(dve_chain, steps[0])

            four = [P, BT, SEC, PRIM]

            def choose(n, b, oh, w8):
                link(V.tensor_reduce(best[:], cand[:], AX, ALU.max))
                link(V.tensor_tensor(pick[:], cand[:], best[:, :, :, None].to_broadcast(four), ALU.is_equal))
                link(V.tensor_tensor(pick[:], pick[:], rank[:, None, None, :].to_broadcast(four), ALU.mult))
                V.tensor_scalar(best[:], best[:], 0.5, None, ALU.is_ge)
                link(V.tensor_reduce(gain[:], pick[:], AX, ALU.max))
                V.tensor_tensor(moved[:], best[:], w8[:, :, PRIM:TOP], ALU.mult)
                link(V.tensor_tensor(pick[:], pick[:], gain[:, :, :, None].to_broadcast(four), ALU.is_equal))
                V.tensor_tensor(slot_w[:, :, PRIM:TOP], w8[:, :, PRIM:TOP], moved[:], ALU.subtract)
                link(V.tensor_tensor(pick[:], pick[:], moved[:, :, :, None].to_broadcast(four), ALU.mult))
                link(V.tensor_reduce(gain[:], pick[:].rearrange("p i j k -> p i k j"), AX, ALU.add))
                link(V.tensor_tensor(slot_w[:, :, 0:PRIM], w8[:, :, 0:PRIM], gain[:], ALU.add))

            def compare(me, i, oh):
                prod4 = prod.rearrange("p (j k e) -> p j k e", j=SEC, k=PRIM)
                rows = job_bank(me)[:, 0:P].rearrange("p (j e) -> p j e", j=SEC)
                V.tensor_tensor(prod4, rows[:, :, None, :].to_broadcast([P, SEC, PRIM, E]),
                                oh[:, i, None, 0:PRIM, :].to_broadcast([P, SEC, PRIM, E]), ALU.mult)\
                    .then_inc(drained_sem(me), 1)
                drained(dve, me)
                link(V.tensor_reduce(cand[:, i], prod4, AX, ALU.add))

            def step(name, n):
                me = (name, n)
                b, oh, w8 = n % B, onehot[:], top[:]
                if name == "PREP":
                    dve.wait_ge(job_copied, COPY[me] + 1)
                    o, i = prep_out(wgu_lo, wd_lo, n, job_bank(me))
                    o_hi, _ = prep_out(wgu_hi, wd_hi, n, job_bank(me))
                    V.tensor_tensor(o, i, o_hi.bitcast(f32), ALU.subtract).then_inc(drained_sem(me), 1)
                elif name == "GW":
                    dve.wait_ge(job_copied, COPY[me] + 1)
                    V.tensor_tensor(gw_lo[:].rearrange("p k e -> p (k e)"), job_bank(me)[:, 0:KC * E],
                                    gw_hi[:].rearrange("p k e -> p (k e)").bitcast(f32), ALU.subtract)\
                        .then_inc(drained_sem(me), 1)
                elif name == "LNa":
                    if n < B:
                        dve.wait_ge(x_loaded[b], 16)
                    elif n < 2 * B:
                        dve.wait_ge(x_added, PHASE * (b + 1))
                    else:
                        drained(dve, ("OU2", b))
                    for i in range(BT):
                        ins = V.bn_stats(stats[:, i, :], x[:, BT * b + i, :])
                    link(ins)
                    for i in range(BT):
                        ins = V.bn_aggr(mv[:, i, :], stats[:, i, :])
                    link(ins)
                    V.tensor_scalar(var_eps[:], mv[:, :, 1], EPS, None, ALU.add).then_inc(var_ready, 1)
                elif name == "LNb":
                    dve.wait_ge(rstd_ready, SEQ[me] + 1)
                    work_free(dve, me)
                    for i in range(BT):
                        ins = V.tensor_scalar(xn[:, i, :], x[:, BT * b + i, :], mv[:, i, 0:1], rstd[:, i:i + 1],
                                              ALU.subtract, ALU.mult)
                    ins.then_inc(xn_ready, 1)
                elif name == "LNc":
                    dve.wait_ge(job_copied, COPY[me] + 1)
                    cols = slice(T * b, T * (b + 1))
                    V.tensor_tensor(xt_lo[:, :, cols], job_bank(me).rearrange("p (k n) -> p k n", k=KC),
                                    xt_hi[:, :, cols].bitcast(f32), ALU.subtract).then_inc(drained_sem(me), 1)
                    drained(dve, me)
                elif name == "R1t":
                    filled(dve, me)
                    logits = job_bank(me)[:, 0:BT * E].rearrange("p (i e) -> p i e", i=BT)
                    link(V.tensor_reduce(pmax[:], logits, AX, ALU.max))
                    V.tensor_tensor(pr[:], logits, pmax[:, :, None].to_broadcast([P, BT, E]), ALU.subtract)\
                        .then_inc(drained_sem(me), 1)
                elif name == "R1b":
                    dve.wait_ge(router_exp, n + 1)
                    for i in range(BT):
                        ins = V.max(w8[:, i, :], pr[:, i, :])
                    link(ins)
                    for i in range(BT):
                        ins = V.max_index(top_i[:, i, :], w8[:, i, :], pr[:, i, :])
                    link(ins)
                    V.tensor_reduce(total[:], pr[:], AX, ALU.add)
                    link(V.tensor_copy(top_f[:], top_i[:]))
                    link(V.reciprocal(total[:], total[:]))
                elif name == "R1c":
                    if n == 0:
                        dve.wait_ge(consts_ready, 1)
                    for part_ in (slice(PRIM, TOP), slice(0, PRIM)):
                        ins = V.tensor_tensor(oh[:, :, part_], top_f[:, :, part_, None].to_broadcast([P, BT, PRIM, E]),
                                              iota[:, None, None, :].to_broadcast([P, BT, PRIM, E]), ALU.is_equal)
                        if part_.start == PRIM:
                            ins.then_inc(onehot_ready, 1)
                    link(V.tensor_tensor(w8, w8, total[:, :, None].to_broadcast([P, BT, TOP]), ALU.mult))
                    link(V.tensor_reduce(total[:], w8, AX, ALU.add))
                    link(V.tensor_scalar(total[:], total[:], 1e-12, None, ALU.max))
                    link(V.reciprocal(total[:], total[:]))
                    link(V.tensor_tensor(w8, w8, total[:, :, None].to_broadcast([P, BT, TOP]), ALU.mult))
                elif name[0:3] == "R2b":
                    filled(dve, me)
                    work_free(dve, me)
                    compare(me, int(name[3]), oh)
                elif name == "R2c":
                    choose(n, b, oh, w8)
                elif name == "R2d":
                    work_free(dve, me)
                    prod8 = prod.rearrange("p (i k e) -> p i k e", i=BT, k=TOP)
                    link(V.tensor_tensor(prod8, oh, slot_w[:, :, :, None].to_broadcast([P, BT, TOP, E]), ALU.mult))
                    V.tensor_reduce(cw[:, BT * b:BT * (b + 1), :], prod8.rearrange("p i k e -> p i e k"), AX, ALU.add)\
                        .then_inc(cw_ready, 1)
                    dve.wait_ge(cw_ready, n + 1)
                elif name == "QK":
                    dve.wait_ge(job_copied, COPY[me] + 1)
                    V.scalar_tensor_tensor(q_lo, job_bank(me, 0), D ** -0.5, q_hi.bitcast(f32),
                                           ALU.mult, ALU.subtract).then_inc(drained_sem(me, 0), 1)
                    filled(dve, me, 1)
                    if n == 0:
                        dve.wait_ge(attn_w_ready, 1)
                    if n >= 2:
                        dve.wait_ge(probs_used, HP * (n - 1))
                    dve.wait_ge(v_t_ready, n + 1)
                    kv = job_bank(me, 1)
                    o = base(n)
                    link(V.tensor_copy(ks[o:o + 3 * D, :], kv[o:o + 3 * D, 0:T]))
                    low = slice(o + 2 * D, o + 3 * D)
                    V.tensor_tensor(ks[low, :], kv[low, 0:T], ks[low, :].bitcast(f32), ALU.subtract)\
                        .then_inc(drained_sem(me, 1), 1)
                elif name == "VT":
                    filled(dve, me)
                    if n >= 1:
                        dve.wait_ge(v_ready, n)
                    flipped = job_bank(me)[:, 0:BT * 2 * D].rearrange("p (i d) -> p i d", i=BT)
                    V.tensor_copy(v_raw[:], flipped[:, :, D:2 * D]).then_inc(drained_sem(me), 1)
                elif name == "SMT":
                    dve.wait_ge(job_copied, COPY[me] + 1)
                    if n >= 1:
                        filled(dve, ("OU1", n - 1))
                    V.scalar_tensor_tensor(neg_lo, job_bank(me)[0:H, 0:T], SHIFT, neg_hi.bitcast(f32),
                                           ALU.add, ALU.subtract).then_inc(drained_sem(me), 1)
                elif name[0:2] == "SM":
                    i, hh, heads, _ = sm_chunk(int(name[2:]))
                    filled(dve, me)
                    V.tensor_reduce(neg_max[:, i, hh:hh + heads], job_bank(me).rearrange("p (a n) -> p a n", a=heads),
                                    AX, ALU.max, negate=True).then_inc(drained_sem(me), 1)
                elif name[0:3] == "OUn":
                    g = int(name[3])
                    dve.wait_ge(probs_used, HP * n + (g + 1) * HG // 2)
                    if g == 0:
                        dve.wait_ge(max_moved, 32 * (n + 1))
                    V.tensor_reduce(summed[:].rearrange("p i h d -> p (i h) d"),
                                    pv[:, :, :, 0:3 * D].rearrange("p i h (m d) -> p (i h) d m", m=3), AX, ALU.add)
                    link(V.reciprocal(rsum[:], pv[:, :, :, 3 * D]))
                    V.tensor_tensor(attn[:, :, g * HG * D:(g + 1) * HG * D].rearrange("p i (h d) -> p i h d", h=HG),
                                    summed[:], rsum[:, :, :, None].to_broadcast([P, BT, HG, D]), ALU.mult)\
                        .then_inc(pv_read, 1)
                elif name == "OU2":
                    filled(dve, me)
                    tiles = slice(BT * n, BT * (n + 1))
                    V.tensor_tensor(x[:, tiles, :], job_bank(me).rearrange("p (i c) -> p i c", i=BT), x[:, tiles, :],
                                    ALU.add).then_inc(drained_sem(me), 1)

            def weigh(a, u, b, g, i, loop):
                if isinstance(u, int) and u % PHASE == 0 and a == 0:
                    dve.wait_ge(cw_ready, u // PHASE + 1)
                dve.wait_ge(gate_done, u * 2 + a + 1)
                src = gu_banks[(2 * i + a) if loop else (2 * u + a) % GU_BANKS]
                if isinstance(u, int) and u in TANH_SLOTS:
                    gate_cols = src[:, 0:HC].rearrange("p (e n) -> p e n", e=2)[:, :, 0:F]
                    both = h[:, i, 2 * a:2 * a + 2, :]
                    link(V.scalar_tensor_tensor(both, both, 1.0, gate_cols, ALU.add, ALU.mult))
                for e in range(2 * a, 2 * a + 2):
                    up = src[:, (e % 2) * 2 * F + F:(e % 2 + 1) * 2 * F]
                    ins = V.scalar_tensor_tensor(h[:, i, e, :], h[:, i, e, :], cw[:, BT * b + i, bass.ds(g * EG + e, 1)],
                                                 up, ALU.mult, ALU.mult)
                ins.then_inc(h_ready, 1)

            def keep_lo(u, i):
                dve.wait_ge(ht_hi_ready, u + 1)
                if not (isinstance(u, int) and u < 2):
                    dve.wait_ge(dn_done, u - 1)
                V.tensor_tensor(ht_lo[:, i, :], tr_bank[:, 0:FC * P], ht_hi[:, i, :].bitcast(f32),
                                ALU.subtract).then_inc(ht_ready, 1)

            def add(u, t):
                half = 0.25 if isinstance(u, int) and u in TANH_SLOTS else 0.5
                dve.wait_ge(dn_done, u + 1)
                if not (isinstance(u, int) and u < 2):
                    dve.wait_ge(x_added, u - 1)
                V.scalar_tensor_tensor(x[:, t, :], dn_bank[:, 0:C], half, x[:, t, :], ALU.mult, ALU.add).then_inc(x_added, 1)

            def part(q, u, b, g, i, loop):
                if q < 2:
                    weigh(q, u, b, g, i, loop)
                elif q == 2 and not (isinstance(u, int) and u < 1):
                    keep_lo(u - 1, 1 - i)
                elif q == 3 and not (isinstance(u, int) and u < 2):
                    b2 = phase_of(u - 2)[0] if isinstance(u, int) else b
                    add(u - 2, BT * b2 + i)

            def plain_group(u0, b, g0):
                with dve.Fori(g0, G) as g:
                    for i in range(BT):
                        for q in range(PARTS):
                            part(q, g * BT + (u0 + i), b, g, i, True)

            def last():
                keep_lo(ALL - 1, 1)
                add(ALL - 2, NT - 2)
                add(ALL - 1, NT - 1)

            walk(part, step, plain_group, last)

        @block.tensor
        def _(pe):
            def mm(out_, lhs, rhs, start, stop, **kw):
                return nc.tensor.matmul(out_, lhs, rhs, start=start, stop=stop, **kw)

            def claim(step, i=0):
                _, bank_, before, batches = JOB[step, i]
                if before:
                    pe.wait_ge(job_drained[bank_], before)
                if bank_ == 2 and batches:
                    pe.wait_ge(pv_read, H // HG * batches)
                return job_banks[bank_][:, :]

            def split_product(out_, parts):
                for m, (lhs, rhs) in enumerate(parts):
                    ins = mm(out_, lhs, rhs, m == 0, m == len(parts) - 1)
                return ins

            def three(a_hi, a_lo, b_hi, b_lo):
                return [(a_lo, b_hi), (a_hi, b_lo), (a_hi, b_hi)]

            def step(name, n):
                me = (name, n)
                b = n % B
                cols = slice(T * b, T * (b + 1))
                tok = [slice(T * b + i * P, T * b + (i + 1) * P) for i in range(BT)]
                if name == "PREP":
                    if n % STEPS == 0:
                        pe.wait_ge(gu_loaded, 16 * (n // STEPS + 1))
                    if n % STEPS == RB // 2:
                        pe.wait_ge(d_loaded, 16 * KC * (n // STEPS + 1))
                    dst = claim(me)
                    for raw, place in prep_parts(n % STEPS, dst):
                        ins = nc.tensor.transpose(place, raw, ident[:])
                    ins.then_inc(job_filled, 1)
                elif name == "GW":
                    pe.wait_ge(ident_ready, 1)
                    pe.wait_ge(gate_loaded, 16)
                    dst = claim(me)
                    for k in range(KC):
                        ins = nc.tensor.transpose(dst[:, k * E:(k + 1) * E], attn[0:E, 0, k * P:(k + 1) * P], ident[0:E, 0:E])
                    ins.then_inc(job_filled, 1)
                elif name == "LNc":
                    dst = claim(me)
                    pe.wait_ge(xn_ready, SEQ[me] + 1)
                    for k in range(KC):
                        for i in range(BT):
                            ins = nc.tensor.transpose(dst[:, (k * BT + i) * P:(k * BT + i + 1) * P],
                                                      xn[:, i, k * P:(k + 1) * P], ident[:])
                    ins.then_inc(job_filled, 1)
                elif name == "R1a":
                    dst = claim(me)
                    ln = ("LNc", n if n < B else n + B)
                    pe.wait_ge(job_copied, COPY[ln] + 1)
                    if n == 0:
                        drained(pe, ("GW", 0))
                    for m, (a, w) in enumerate(((xt_hi, gw_lo), (xt_hi, gw_hi), (xt_lo, gw_hi))):
                        if m == 2:
                            drained(pe, ln)
                        for k in range(KC):
                            ins = mm(dst[0:E, 0:T], w[:, k, :], a[:, k, cols], m == k == 0, m == 2 and k == KC - 1)
                    ins.then_inc(job_filled, 1)
                elif name == "R1t":
                    dst = claim(me)
                    drained(pe, ("R1a", n))
                    for i in range(BT):
                        ins = nc.tensor.transpose(dst[:, i * E:(i + 1) * E], logits_t[:, i * P:(i + 1) * P], ident[0:E, 0:E])
                    ins.then_inc(job_filled, 1)
                elif name == "R2a":
                    flipped = claim(me)[:, 0:P].bitcast(bf16)
                    if n == 0:
                        pe.wait_ge(consts_ready, 1)
                    pe.wait_ge(onehot_ready, n + 1)
                    for i in range(BT):
                        ins = nc.tensor.transpose(flipped[:, i * P:(i + 1) * P],
                                                  onehot[:, i, PRIM:TOP, :].rearrange("p k e -> p (k e)"), ident_b[:])
                    ins.then_inc(job_filled, 1)
                elif name[0:3] == "R2b":
                    dst = claim(me)
                    drained(pe, ("R2a", n))
                    mm(dst[:, 0:P], onehot_t[:, int(name[3]), :], sim_bd[:], True, True).then_inc(job_filled, 1)
                elif name == "QK":
                    dst = claim(me, 0)
                    drained(pe, ("LNc", B + n))
                    if n == 0:
                        pe.wait_ge(attn_w_ready, 1)
                    for blk in range(H // HB):
                        w = slice(blk * P, (blk + 1) * P)
                        ins = split_product(dst[:, blk * T:(blk + 1) * T],
                                            [p_ for k in range(KC) for p_ in
                                             three(wq_hi[:, k, w], wq_lo[:, k, w], xt_hi[:, k, cols], xt_lo[:, k, cols])])
                    ins.then_inc(job_filled, 1)
                    dst = claim(me, 1)
                    ins = split_product(dst[:, 0:T], [p_ for k in range(KC) for p_ in
                                                      three(wkv_hi[:, k, :], wkv_lo[:, k, :],
                                                            xt_hi[:, k, cols], xt_lo[:, k, cols])])
                    ins.then_inc(job_filled, 1)
                elif name == "VT":
                    dst = claim(me)
                    pe.wait_ge(v_t_ready, n + 1)
                    for i in range(BT):
                        ins = nc.tensor.transpose(dst[:, i * 2 * D:(i + 1) * 2 * D], v_t[:, i * P:(i + 1) * P],
                                                  ident[P - 2 * D:P, P - 2 * D:P])
                    ins.then_inc(job_filled, 1)
                elif name == "SMT":
                    dst = claim(me)
                    for m in (SMS - 2, SMS - 1):
                        drained(pe, (f"SM{m}", n))
                    for i in range(BT):
                        ins = nc.tensor.transpose(dst[0:H, i * P:(i + 1) * P], neg_max[:, i, :], ident[:])
                    ins.then_inc(job_filled, 1)
                elif name[0:2] == "SM":
                    if name == "SM0":
                        pe.wait_ge(q_moved, 16 * MOVES * (n + 1))
                        drained(pe, ("QK", n), 1)
                    rows = slice(base(n), base(n) + 3 * D)
                    i, hh, heads, width = sm_chunk(int(name[2:]))
                    dst = claim(me)
                    mm(dst.rearrange("p (a n) -> p a n", a=heads)[:, :, width - P:width], hide_q[:],
                       ident_b[:, None, :].to_broadcast([P, heads, P]), True, False, skip_group_check=True)
                    for a in range(heads):
                        ins = mm(dst[:, a * width:(a + 1) * width], qs[rows, hh + a, i * P:(i + 1) * P],
                                 ks[rows, 0:width], False, a == heads - 1, skip_group_check=True)
                    ins.then_inc(job_filled, 1)
                elif name[0:2] == "PS":
                    scores(n, int(name[2:]))
                elif name[0:2] == "PV":
                    times_v(n, int(name[2:]))
                elif name == "OU1":
                    dst = claim(me)
                    pe.wait_ge(pv_read, H // HG * (n + 1))
                    for i in range(BT):
                        for k in range(KC):
                            ins = nc.tensor.transpose(dst[:, (i * KC + k) * P:(i * KC + k + 1) * P],
                                                      attn[:, i, k * P:(k + 1) * P], ident[:])
                    ins.then_inc(job_filled, 1)
                elif name == "OU2":
                    dst = claim(me)
                    if n == 0:
                        pe.wait_ge(wo_loaded, 32)
                    drained(pe, ("OU1", n))
                    for i in range(BT):
                        cols = slice(i * C, (i + 1) * C)
                        mm(dst[:, cols], ones_row, bo_row, True, False)
                        for k in range(KC):
                            ins = mm(dst[:, cols], attn_t[:, i, k * P:(k + 1) * P], wo_sb[:, k, :], False, k == KC - 1)
                    ins.then_inc(job_filled, 1)

            def scores(n, w):
                me = (f"PS{w}", n)
                if w == 0:
                    pe.wait_ge(max_moved, 32 * (n + 1))
                rows = slice(base(n), base(n) + 3 * D + 2)
                heads = slice(2 * w, 2 * w + 2)
                diagonal = ident_b[:, None, :].to_broadcast([P, 2, P])
                dst = claim(me, 0).rearrange("p (a n) -> p a n", a=2)
                mm(dst[:, :, 0:P], hide_k[:], diagonal, True, False, skip_group_check=True)
                mm(dst, ks[rows, 0:P], qs[rows, heads, :], False, True, skip_group_check=True).then_inc(job_filled, 1)
                dst = claim(me, 1)[:, 0:2 * P].rearrange("p (a n) -> p a n", a=2)
                mm(dst, hide_k[:], diagonal, True, False, skip_group_check=True)
                mm(dst, ks[rows, P:T], qs[rows, heads, P:T], False, True, skip_group_check=True).then_inc(job_filled, 1)

            def times_v(n, w):
                pe.wait_ge(p_ready, HP * n + w + 1)
                if w == 0:
                    pe.wait_ge(v_ready, n + 1)
                    pe.wait_ge(job_drained[2], PV_JOBS[n])
                if 2 * w % HG == 0 and HP * n + w > 0:
                    pe.wait_ge(pv_read, (HP * n + w) * 2 // HG)
                v = [v3[:, n % 2, i, :] for i in range(BT)]
                for a in range(2):
                    hh = (2 * w + a) % HG
                    blocks = ((0, a * T, 0), (1, a * T + P, 0), (1, 2 * T + a * P, 1))
                    for i, at, keys in blocks:
                        mm(pv[:, i, hh, :], p_hi[:, at:at + P], v[keys], keys == 0, False)
                        ins = mm(pv[:, i, hh, :], p_lo[:, at:at + P], v[keys], False, i == keys)
                ins.then_inc(probs_used, 1)

            def gate_up_products(a, u, b, g, i, loop):
                if a == 0 and isinstance(u, int) and u % PHASE == 0:
                    drained(pe, ("LNc", (u // PHASE) if u < B * PHASE else B + u // PHASE))
                if isinstance(u, int) and u < PHASE and i == 0:
                    for s in range(RB // 2):
                        drained(pe, ("PREP", STEPS * g + s))
                t = BT * b + i
                tok = slice(t * P, (t + 1) * P)
                if loop:
                    if isinstance(u, int) and u == PLAIN:
                        pe.wait_ge(h_ready, 2 * u)
                    pe.wait_ge(h_ready, u * 2 + (a - GU_BANKS))
                    dst = gu_banks[2 * i + a]
                else:
                    if 2 * u + a >= GU_BANKS:
                        pe.wait_ge(h_ready, 2 * u + a - GU_BANKS + 1)
                    dst = gu_banks[(2 * u + a) % GU_BANKS]
                ac = slice(a * HC, (a + 1) * HC)
                ins = split_product(dst[:, 0:HC], [p_ for k in range(KC) for p_ in
                                                   three(xt_hi[:, k, tok], xt_lo[:, k, tok],
                                                         wgu_hi[:, g, k, ac], wgu_lo[:, g, k, ac])])
                ins.then_inc(gu_done, 1)

            def transpose_h(u, i):
                pe.wait_ge(h_ready, u * 2 + 2)
                if not (isinstance(u, int) and u < 1):
                    pe.wait_ge(ht_ready, u)
                flat = h[:, i].rearrange("p e f -> p (e f)")
                for j in range(FC):
                    ins = nc.tensor.transpose(tr_bank[:, j * P:(j + 1) * P], flat[:, j * P:(j + 1) * P], ident[:])
                ins.then_inc(tr_done, 1)

            def down_products(u, g, i):
                if isinstance(u, int) and u < PHASE and i == 0:
                    for s in range(RB // 2, STEPS):
                        drained(pe, ("PREP", STEPS * g + s))
                pe.wait_ge(ht_ready, u + 1)
                if not (isinstance(u, int) and u < 1):
                    pe.wait_ge(x_added, u)
                ins = split_product(dn_bank[:, 0:C], [p_ for j in range(FC) for p_ in
                                                      three(ht_hi[:, i, j * P:(j + 1) * P], ht_lo[:, i, j * P:(j + 1) * P],
                                                            wd_hi[:, g, j, :], wd_lo[:, g, j, :])])
                ins.then_inc(dn_done, 1)

            def part(q, u, b, g, i, loop):
                if q < 2:
                    gate_up_products(q, u, b, g, i, loop)
                elif q == 2 and not (isinstance(u, int) and u < 1):
                    transpose_h(u - 1, 1 - i)
                elif q == 3 and not (isinstance(u, int) and u < 2):
                    down_products(u - 2, phase_of(u - 2)[1] if isinstance(u, int) else g - 1, i)

            def plain_group(u0, b, g0):
                if u0 + g0 * BT == PLAIN:
                    pe.wait_ge(h_ready, 2 * PLAIN)
                with pe.Fori(g0, G) as g:
                    for i in range(BT):
                        for q in range(PARTS):
                            part(q, g * BT + (u0 + i), b, g, i, True)

            def last():
                transpose_h(ALL - 1, 1)
                down_products(ALL - 2, G - 1, 0)
                down_products(ALL - 1, G - 1, 1)

            walk(part, step, plain_group, last)


_INS = ["L0_attn_x", "L0_attn_Wq", "L0_attn_Wk", "L0_attn_Wv", "L0_attn_Wo", "L0_attn_bo",
        "L0_ffn_gate_weight", "L0_ffn_gate_up_proj", "L0_ffn_down_proj", "L0_ffn_similarity"]


def kernel(**inputs):
    import numpy as _np
    import concourse.bacc as _bacc
    from concourse import mybir as _mybir
    from concourse.bass_utils import run_bass_kernel_spmd as _run

    nc = _bacc.Bacc("TRN2", target_bir_lowering=False, num_devices=1, dynamic_dma_scratch_size=256)
    arrays, args = {}, []
    for name in _INS:
        a = _np.ascontiguousarray(inputs[name])
        arrays[f"in_{name}"] = a
        args.append(nc.dram_tensor(f"in_{name}", a.shape, _mybir.dt.from_np(a.dtype), kind="ExternalInput").ap())
    args.append(nc.dram_tensor("out_x", (B, T, C), _mybir.dt.float32, kind="ExternalOutput").ap())
    macaron(nc, *args)
    r = _run(nc, [arrays], core_ids=[0])
    return r.results[0]["out_x"]
```
